# Optimizing a Trainium2 kernel written in Bass

```python
import numpy as np
import jax
import jax.numpy as jnp

def _softmax(x, axis=-1):
    return jax.nn.softmax(x, axis=axis)

def _gelu(x):
    return jax.nn.gelu(x, approximate=True)

def _silu(x):
    return jax.nn.silu(x)

def _sigmoid(x):
    return jax.nn.sigmoid(x)

def _layernorm(x, axis=-1, eps=1e-05):
    m = jnp.mean(x, axis=axis, keepdims=True)
    v = jnp.var(x, axis=axis, keepdims=True)
    return (x - m) / jnp.sqrt(v + eps)

def _scatter_add(tgt, idx, src, axis=0):
    return tgt.at[idx].add(src)

def _segment_sum(src, seg, n):
    return jax.ops.segment_sum(src, seg, n)
kernel_name = 'mk_gnn_preln_d1_gnn_r64_e48b2e'

def setup_inputs(seed: int=0):
    np.random.seed(seed)
    _w = jnp.asarray

    def _rec_inputs():
        import jax
        import jax.numpy as jnp
        _gk = jax.random.key(seed)
        x = -0.0005121 + 1.001 * jax.random.normal(jax.random.fold_in(_gk, 1), (100000, 64), jnp.float32)
        src = jax.random.randint(jax.random.fold_in(_gk, 2), (25000,), 0, 100000, jnp.int32)
        dst = jax.random.randint(jax.random.fold_in(_gk, 3), (25000,), 0, 100000, jnp.int32)
        _o = jnp.argsort(dst, stable=True)
        src = src[_o]
        dst = dst[_o]
        edge_attr_64 = -6.74381e-05 + 0.999835 * jax.random.normal(jax.random.fold_in(_gk, 11), (25000, 64), jnp.float32)
        return (x, src, dst, edge_attr_64)
    x, src, dst, edge_attr_64 = _rec_inputs()

    def _L0_gnn_setup():
        import jax, jax.numpy as jnp
        import numpy as np
        N_NODES = 50000
        N_EDGES = 1250000
        D_NODE = 64
        D_EDGE = 64
        M_OUT = 64
        U_OUT = 64
        key = jax.random.key(seed)
        k1, k2, k3, k4, k5, k6 = jax.random.split(key, 6)
        H = jax.random.normal(k1, (N_NODES, D_NODE), dtype=jnp.float32)
        Xe = jax.random.normal(k2, (N_EDGES, D_EDGE), dtype=jnp.float32)
        id_Xe = jax.random.randint(k3, (2, N_EDGES), 0, N_NODES, dtype=jnp.int64)
        M_W = jax.random.normal(k4, (M_OUT, D_NODE + D_EDGE), dtype=jnp.float32) * 0.05
        M_b = jnp.zeros((M_OUT,), dtype=jnp.float32)
        U_W = jax.random.normal(k5, (U_OUT, D_NODE + M_OUT), dtype=jnp.float32) * 0.05
        U_b = jnp.zeros((U_OUT,), dtype=jnp.float32)
        return {'H': H, 'Xe': Xe, 'id_Xe': id_Xe, 'M_W': M_W, 'M_b': M_b, 'U_W': U_W, 'U_b': U_b}
    _L0_gnn_all = _L0_gnn_setup()
    _L0_gnn_in = {k: v for k, v in _L0_gnn_all.items() if k in ('M_W', 'M_b', 'U_W', 'U_b')}
    del _L0_gnn_all
    return {'x': x, 'src': src, 'dst': dst, 'edge_attr_64': edge_attr_64, 'L0_gnn_M_W': _L0_gnn_in['M_W'], 'L0_gnn_M_b': _L0_gnn_in['M_b'], 'L0_gnn_U_W': _L0_gnn_in['U_W'], 'L0_gnn_U_b': _L0_gnn_in['U_b']}

def reference(x, src, dst, edge_attr_64, L0_gnn_M_W, L0_gnn_M_b, L0_gnn_U_W, L0_gnn_U_b):
    import jax
    import jax.numpy as jnp

    def _L0_gnn_ref(H, Xe, id_Xe, M_W, M_b, U_W, U_b):
        import jax, jax.numpy as jnp
        import numpy as np
        N_NODES = 50000
        N_EDGES = 1250000
        D_NODE = 64
        D_EDGE = 64
        M_OUT = 64
        U_OUT = 64
        features = H[id_Xe[0]]
        M_in = jnp.concatenate([features, Xe], axis=1)
        Y = jax.nn.relu(M_in @ M_W.T + M_b)
        Z = jax.ops.segment_sum(Y, id_Xe[1], num_segments=H.shape[0])
        U_in = jnp.concatenate([H, Z], axis=1)
        H_next = jax.nn.relu(U_in @ U_W.T + U_b)
        return H_next
    edge_index = jnp.stack([src, dst])
    h = jnp.maximum(_layernorm(x, axis=-1), 0.0)
    x = x + _L0_gnn_ref(h, edge_attr_64, edge_index, L0_gnn_M_W, L0_gnn_M_b, L0_gnn_U_W, L0_gnn_U_b)
    return x

_drawn_inputs = setup_inputs


def setup_inputs(seed=0):
    import zlib

    import numpy as np

    out = dict(_drawn_inputs(seed))
    spreads = {'L0_gnn_M_b': (0.0, 0.741), 'L0_gnn_U_b': (0.0, 0.1)}
    factors = {}
    for name, (base, spread) in spreads.items():
        noise = np.random.default_rng([zlib.crc32(name.encode()), seed]).standard_normal(out[name].shape)
        drawn = base * np.exp(spread * noise) if base else spread * noise
        out[name] = jnp.asarray(drawn.astype(out[name].dtype))
    for name, factor in factors.items():
        out[name] = (out[name] * factor).astype(out[name].dtype)
    return out
```

```python
import concourse.bass as bass
from concourse import mybir
from concourse.alu_op_type import AluOpType as ALU
from contextlib import ExitStack

F32 = mybir.dt.float32
I32 = mybir.dt.int32
ACT = mybir.ActivationFunctionType
AX = mybir.AxisListType

P = 128
D = 64
EPS = 1e-5


def gnn_kernel(nc, x, src, dst, edge_attr, M_W, M_b, U_W, U_b, out):
    N = x.shape[0]
    E = src.shape[0]

    G = 8
    GROUP = 2 * P
    CHUNK = G * GROUP
    CHUNKS = N // CHUNK
    HEAD = N - CHUNKS * CHUNK
    HEAD_G = HEAD // GROUP
    HEAD_P = (HEAD - HEAD_G * GROUP) // 2
    R = 2 * G
    HALF = R // 2 * D
    NX = 4
    assert CHUNKS % NX == 0 and HEAD % 2 == 0

    J = 8
    BLOCK = P * J
    BLOCKS = -(-E // BLOCK)
    REST_P = (E - (BLOCKS - 1) * BLOCK) // J
    assert REST_P * J == E - (BLOCKS - 1) * BLOCK and BLOCKS % 2 == 1
    YW = D + 4
    TILES = -(-E // P)
    FAR = float(1 << 20)

    ctx = ExitStack()
    with ctx:
        def sb(name, shape, dt=F32):
            return ctx.enter_context(nc.sbuf_tensor(name, shape, dt))

        given = []

        def sem(name, n=0):
            s = ctx.enter_context(nc.semaphore(name))
            if n:
                given.append((s, n))
            return s

        def over(s, n):
            return n + sum(g for t, g in given if t is s)

        messages = nc.dram_tensor("messages", [BLOCKS * BLOCK, YW], F32, kind="Internal").ap()
        table = nc.dram_tensor("table", [(CHUNKS + 1) * CHUNK, D], F32, kind="Internal").ap()

        column = sb("column", [P, P])
        row = sb("row", [P, 1])
        ident = sb("ident", [P, P])
        below = sb("below", [P, P])
        eps_t = sb("eps_t", [P, 1])
        weight_in = sb("weight_in", [P, 4, P])
        weight = sb("weight", [P, 4, P])
        MH, ME, UH, UZ = range(4)
        msg_bias = sb("msg_bias", [P, 1])
        node_bias = sb("node_bias", [P, R * D])
        node_bias_row = sb("node_bias_row", [P, D])

        xs = [sb(f"xs{k}", [P, R, D]) for k in range(NX)]
        xc = [sb(f"xc{k}", [P, R, D]) for k in range(2)]
        sq = sb("sq", [P, R, D])
        total = sb("total", [P, R])
        var = sb("var", [P, R])
        dev = sb("dev", [P, R])
        rdev = sb("rdev", [P, R])
        hT = [sb(f"hT{k}", [P, 2, HALF]) for k in range(2)]
        tab = [sb(f"tab{k}", [P, R, D]) for k in range(2)]
        res = [sb(f"res{k}", [P, R, D]) for k in range(2)]

        src_i = [sb(f"src_i{k}", [P, J], I32) for k in range(2)]
        dst_i = [sb(f"dst_i{k}", [P, J], I32) for k in range(2)]
        xg = [sb(f"xg{k}", [P, J, D]) for k in range(2)]
        ea = [sb(f"ea{k}", [P, J, D]) for k in range(2)]
        hg = sb("hg", [P, J, D])
        sqg = sb("sqg", [P, J, D])
        total_g = sb("total_g", [P, J])
        var_g = sb("var_g", [P, J])
        dev_g = sb("dev_g", [P, J])
        rdev_g = sb("rdev_g", [P, J])
        hgT = sb("hgT", [P, J * D])
        eaT = sb("eaT", [P, J * D])
        msgT = sb("msgT", [P, J * D])
        ys = [sb(f"ys{k}", [P, J, YW]) for k in range(2)]

        yt = sb("yt", [P, YW])
        dcol = sb("dcol", [P, P])
        same = sb("same", [P, P])
        earlier = sb("earlier", [P, P])
        n_before = sb("n_before", [P, 1])
        at_f = sb("at_f", [P, 1])
        read_i = sb("read_i", [P, 1], I32)
        write_i = sb("write_i", [P, 1], I32)
        t_old = sb("t_old", [P, D])
        t_new = sb("t_new", [P, D])

        bank = [ctx.enter_context(nc.psum_tensor(f"bank{k}", [P, 512], F32)) for k in range(8)]
        turned = bank[0:2]
        pre = [bank[2:4], bank[4:6]]
        pa, pb = bank[6], bank[7]

        went = sem("went")

        const_ready = sem("const_ready")
        ident_ready = sem("ident_ready")
        weight_cleared = sem("weight_cleared")
        weight_loaded = sem("weight_loaded")
        weight_turned = sem("weight_turned")
        weight_ready = sem("weight_ready")
        bias_loaded = sem("bias_loaded")
        bias_ready = sem("bias_ready")
        table_filled = sem("table_filled")

        edge_in = [sem(f"edge_in{k}") for k in range(2)]
        index_cleared = sem("index_cleared")
        gathered = [sem(f"gathered{k}") for k in range(2)]
        g_total = sem("g_total")
        g_centred = sem("g_centred")
        g_squared = sem("g_squared")
        g_node = sem("g_node")
        g_var = sem("g_var")
        g_dev = sem("g_dev")
        g_rdev = sem("g_rdev")
        g_h = sem("g_h")
        e_turned = sem("e_turned")
        h_turned = sem("h_turned", 1)
        eaT_ready = sem("eaT_ready")
        hgT_ready = sem("hgT_ready")
        g_msg = sem("g_msg")
        msgT_ready = sem("msgT_ready", 1)
        g_update = sem("g_update")
        ys_ready = sem("ys_ready", 1)
        ys_stored = [sem(f"ys_stored{k}", 16) for k in range(2)]

        y_loaded = sem("y_loaded")
        y_cols = sem("y_cols")
        y_rows = sem("y_rows")
        y_same = sem("y_same")
        y_earlier = sem("y_earlier")
        y_before = sem("y_before")
        y_at = sem("y_at")
        y_read = sem("y_read")
        y_write = sem("y_write")
        y_sum = sem("y_sum")
        t_cleared = sem("t_cleared")
        t_read = sem("t_read")
        t_summed = sem("t_summed")
        t_written = sem("t_written")

        x_loaded = [sem(f"x_loaded{k}") for k in range(NX)]
        tab_loaded = [sem(f"tab_loaded{k}") for k in range(2)]
        n_total = sem("n_total")
        n_centred = sem("n_centred")
        n_squared = sem("n_squared")
        n_var = sem("n_var", 1)
        n_dev = sem("n_dev")
        n_rdev = sem("n_rdev")
        n_h = sem("n_h")
        n_turned = sem("n_turned", 4)
        hT_ready = sem("hT_ready", 2)
        pre_ready = sem("pre_ready", 4)
        res_ready = sem("res_ready", 4)
        stored = [sem(f"stored{k}", 16) for k in range(2)]

        def node_rows(t, first):
            return t[bass.ds(first, CHUNK), :].rearrange("(g p i) d -> p g (i d)", g=G, i=2)

        def by_group(tile):
            return tile[:].rearrange("p (g i) d -> p g (i d)", i=2)

        def spread(stat, n):
            return stat[:].unsqueeze(2).to_broadcast([P, n, D])

        def edge_loop(engine, step):
            with engine.Fori(0, BLOCKS // 2) as i:
                for k in range(2):
                    step(k, 2 * i + k, i, False)
            step(0, BLOCKS - 1, BLOCKS // 2, True)

        def node_loop(engine, step, begin=0):
            with engine.Fori(0, CHUNKS // NX) as i:
                for k in range(NX):
                    step(begin + k, NX * i + begin + k, i)

        def wait_alone(engine, s, value):
            engine.wait_ge(s, value)
            engine.sem_inc(went, 1)

        block = ctx.enter_context(nc.Block())

        @block.sync
        def _(sp):
            for s, n in given:
                sp.sem_inc(s, n)
            sp.wait_ge(weight_cleared, 1)
            for w, (m, first) in enumerate([(M_W, 0), (M_W, D), (U_W, 0), (U_W, D)]):
                for h in (0, D):
                    sp.dma_start(weight_in[h:h + D, w, h:h + D], m[:, first:first + D]).then_inc(weight_loaded, 16)
            for h in (0, D):
                sp.dma_start(msg_bias[h:h + D, :], M_b.rearrange("(p a) -> p a", a=1)).then_inc(bias_loaded, 16)
            sp.dma_start(node_bias_row[:], U_b.rearrange("(a d) -> a d", a=1).to_broadcast([P, D])).then_inc(bias_loaded, 16)

            def load_edges(b, k, t, n=P):
                if t is not None:
                    wait_alone(sp, gathered[k], 16 * J * t)
                    wait_alone(sp, g_node, b - 1)
                    wait_alone(sp, e_turned, b - 1)
                if n < P:
                    sp.wait_ge(index_cleared, 2)
                for dram, tile in ((src, src_i), (dst, dst_i)):
                    sp.dma_start(tile[k][:n, :], dram[bass.ds(b * BLOCK, n * J)].rearrange("(p j) -> p j", j=J)).then_inc(edge_in[k], 16)
                sp.dma_start(ea[k][:n, :, :], edge_attr[bass.ds(b * BLOCK, n * J), :].rearrange("(p j) d -> p j d", j=J)).then_inc(edge_in[k], 16)

            def store_messages(b, k):
                wait_alone(sp, ys_ready, over(ys_ready, b + 1))
                wait_alone(sp, g_node, b + 1)
                sp.dma_start(messages[bass.ds(b * BLOCK, BLOCK), :].rearrange("(p j) d -> p j d", j=J), ys[k][:]).then_inc(ys_stored[k], 16)

            load_edges(0, 0, None)
            load_edges(1, 1, None)
            with sp.Fori(0, (BLOCKS - 3) // 2) as i:
                for k in range(2):
                    store_messages(2 * i + k, k)
                    load_edges(2 * i + k + 2, k, i + 1)
            store_messages(BLOCKS - 3, 0)
            load_edges(BLOCKS - 1, 0, BLOCKS // 2, REST_P)
            store_messages(BLOCKS - 2, 1)
            store_messages(BLOCKS - 1, 0)

            sp.wait_ge(bias_ready, 1)
            for c in range(CHUNKS + 1):
                sp.dma_start(table[c * CHUNK:(c + 1) * CHUNK, :].rearrange("(p r) d -> p (r d)", p=P), node_bias[:]).then_inc(table_filled, 16)
            sp.wait_ge(ys_stored[0], over(ys_stored[0], 16 * (BLOCKS // 2 + 1)))
            sp.wait_ge(ys_stored[1], over(ys_stored[1], 16 * (BLOCKS // 2)))
            sp.wait_ge(table_filled, 16 * (CHUNKS + 1))
            sp.dma_start(yt[:], messages[0:P, :]).then_inc(y_loaded, 16)
            with sp.Fori(1, TILES) as t:
                wait_alone(sp, t_written, 16 * t)
                sp.dma_start(yt[:], messages[bass.ds(t * P, P), :]).then_inc(y_loaded, 16)
            sp.wait_ge(t_written, 16 * TILES)

            def load_nodes(n, k, first, used):
                if used:
                    wait_alone(sp, res_ready, over(res_ready, 2 * (n - NX + 1)))
                sp.dma_start(by_group(xs[k]), node_rows(x, first)).then_inc(x_loaded[k], 16)

            def load_table(n, k, first):
                wait_alone(sp, pre_ready, over(pre_ready, 2 * (n - 1)))
                sp.dma_start(by_group(tab[k]), node_rows(table, first)).then_inc(tab_loaded[k], 16)

            for n in range(NX):
                load_nodes(n, n, HEAD + n * CHUNK, False)
            for n in range(2):
                load_table(n, n, HEAD + n * CHUNK)
            with sp.Fori(0, CHUNKS // NX - 1) as i:
                for k in range(NX):
                    n = NX * i + k
                    load_table(n + 2, k % 2, HEAD + (n + 2) * CHUNK)
                    load_nodes(n + NX, k, HEAD + (n + NX) * CHUNK, True)
            for n in range(CHUNKS - NX + 2, CHUNKS):
                load_table(n, n % 2, HEAD + n * CHUNK)
            load_nodes(CHUNKS, 0, 0, True)
            load_table(CHUNKS, 0, 0)

        @block.gpsimd
        def _(pool):
            nc.gpsimd.memset(weight_in[:], 0.0).then_inc(weight_cleared, 1)
            nc.gpsimd.iota(column[:], pattern=[[1, P]], base=0, channel_multiplier=0, allow_small_or_imprecise_dtypes=True).then_inc(const_ready, 1)
            nc.gpsimd.iota(row[:], pattern=[[0, 1]], base=0, channel_multiplier=1, allow_small_or_imprecise_dtypes=True).then_inc(const_ready, 1)

            def gather(k, b, t, used=True):
                pool.wait_ge(edge_in[k], 48 * (t + 1))
                if used:
                    pool.wait_ge(g_centred, b - 1)
                pool.sem_inc(went, 1)
                for j in range(J):
                    pool.indirect_dma_start(out=xg[k][:, j, :], out_offset=None, in_=x[:, :],
                                            in_offset=bass.IndirectOffsetOnAxis(ap=src_i[k][:, j:j + 1], axis=0)).then_inc(gathered[k], 16)

            gather(0, 0, 0, False)
            gather(1, 1, 0, False)
            with pool.Fori(0, BLOCKS // 2 - 1) as i:
                for k in range(2):
                    gather(k, 2 * i + k + 2, i + 1)
            pool.wait_ge(gathered[0], 16 * J * (BLOCKS // 2))
            pool.wait_ge(g_node, BLOCKS - 2)
            nc.gpsimd.memset(src_i[0][:], 0).then_inc(index_cleared, 1)
            nc.gpsimd.memset(dst_i[0][:], int(FAR)).then_inc(index_cleared, 1)
            gather(0, BLOCKS - 1, BLOCKS // 2)

            nc.gpsimd.memset(t_old[:], 0.0).then_inc(t_cleared, 1)
            pool.wait_ge(t_cleared, 1)
            with pool.Fori(0, TILES) as t:
                pool.wait_ge(y_read, t + 1)
                pool.sem_inc(went, 1)
                pool.indirect_dma_start(out=t_old[:], out_offset=None, in_=table[:, :],
                                        in_offset=bass.IndirectOffsetOnAxis(ap=read_i[:], axis=0),
                                        bounds_check=N - 1, oob_is_err=False).then_inc(t_read, 16)
                pool.wait_ge(t_summed, t + 1)
                pool.wait_ge(y_write, t + 1)
                pool.sem_inc(went, 1)
                pool.indirect_dma_start(out=table[:, :], out_offset=bass.IndirectOffsetOnAxis(ap=write_i[:], axis=0),
                                        in_=t_new[:], in_offset=None,
                                        bounds_check=N - 1, oob_is_err=False).then_inc(t_written, 16)

        @block.vector
        def _(dve):
            dve.wait_ge(const_ready, 2)
            nc.vector.tensor_scalar(ident[:], column[:], row[:], None, ALU.is_equal).then_inc(ident_ready, 1)
            nc.vector.tensor_scalar(below[:], column[:], row[:], None, ALU.is_lt).then_inc(ident_ready, 1)
            nc.vector.memset(eps_t[:], EPS).then_inc(ident_ready, 1)
            for k in range(2):
                nc.vector.memset(ys[k][:], 0.0).then_inc(ident_ready, 1)
            dve.wait_ge(weight_turned, 1)
            nc.vector.tensor_copy(weight[:].rearrange("p w c -> p (w c)"), pa[:, :]).then_inc(weight_ready, 1)
            dve.wait_ge(bias_loaded, 48)
            nc.vector.tensor_copy(node_bias[:].rearrange("p (r d) -> p r d", d=D),
                                  node_bias_row[:].unsqueeze(1).to_broadcast([P, R, D])).then_inc(bias_ready, 1)
            dve.wait_ge(ident_ready, 5)

            def edge_norm(k, b, t, last):
                dve.wait_ge(gathered[k], 16 * J * (t + 1))
                nc.vector.tensor_reduce(total_g[:], xg[k][:], AX.X, ALU.add).then_inc(g_total, 1)
                dve.wait_ge(g_total, b + 1)
                dve.wait_ge(h_turned, over(h_turned, b))
                nc.vector.scalar_tensor_tensor(out=hg[:], in0=spread(total_g, J), scalar=-1.0 / D, in1=xg[k][:],
                                               op0=ALU.mult, op1=ALU.add).then_inc(g_centred, 1)
                dve.wait_ge(ys_stored[k], over(ys_stored[k], 16 * t))
                nc.vector.tensor_copy(ys[k][:, :, D:D + 1], dst_i[k][:].unsqueeze(2)).then_inc(g_node, 1)
                dve.wait_ge(g_squared, b + 1)
                nc.vector.tensor_reduce(var_g[:], sqg[:], AX.X, ALU.add).then_inc(g_var, 1)
                dve.wait_ge(g_dev, b + 1)
                nc.vector.reciprocal(rdev_g[:], dev_g[:]).then_inc(g_rdev, 1)
                dve.wait_ge(g_rdev, b + 1)
                nc.vector.tensor_tensor(hg[:], hg[:], spread(rdev_g, J), ALU.mult).then_inc(g_h, 1)

            edge_loop(dve, edge_norm)

            with dve.Fori(0, TILES) as t:
                dve.wait_ge(y_loaded, 16 * t + 16)
                nc.vector.tensor_copy(dcol[:], yt[:, D:D + 1].to_broadcast([P, P])).then_inc(y_cols, 1)
                nc.vector.tensor_copy(read_i[:], yt[:, D:D + 1]).then_inc(y_read, 1)
                dve.wait_ge(y_rows, t + 1)
                nc.vector.tensor_scalar(same[:], pa[:, 0:P], yt[:, D:D + 1], None, ALU.is_equal).then_inc(y_same, 1)
                dve.wait_ge(y_same, t + 1)
                nc.vector.tensor_tensor(earlier[:], same[:], below[:], ALU.mult).then_inc(y_earlier, 1)
                dve.wait_ge(y_earlier, t + 1)
                nc.vector.tensor_reduce(n_before[:], earlier[:], AX.X, ALU.add).then_inc(y_before, 1)
                dve.wait_ge(y_before, t + 1)
                nc.vector.tensor_scalar(at_f[:], n_before[:], 0.0, FAR, ALU.is_gt, ALU.mult).then_inc(y_at, 1)
                dve.wait_ge(y_at, t + 1)
                nc.vector.tensor_tensor(write_i[:], at_f[:], yt[:, D:D + 1], ALU.add).then_inc(y_write, 1)
                dve.wait_ge(y_sum, t + 1)
                dve.wait_ge(t_read, 16 * t + 16)
                nc.vector.tensor_tensor(t_new[:], pb[:, 0:D], t_old[:], ALU.add).then_inc(t_summed, 1)

            def centre(k, n, i):
                dve.wait_ge(x_loaded[k % NX], 16 * (i + 1 + k // NX))
                nc.vector.tensor_reduce(total[:], xs[k % NX][:], AX.X, ALU.add).then_inc(n_total, 1)
                dve.wait_ge(n_total, n + 1)
                dve.wait_ge(n_turned, over(n_turned, 2 * n - 2))
                nc.vector.scalar_tensor_tensor(out=xc[k % 2][:], in0=spread(total, R), scalar=-1.0 / D, in1=xs[k % NX][:],
                                               op0=ALU.mult, op1=ALU.add).then_inc(n_centred, 1)

            def scale(k, n, i):
                dve.wait_ge(n_squared, n + 1)
                nc.vector.tensor_reduce(var[:], sq[:], AX.X, ALU.add).then_inc(n_var, 1)
                dve.wait_ge(n_dev, n + 1)
                nc.vector.reciprocal(rdev[:], dev[:]).then_inc(n_rdev, 1)
                dve.wait_ge(n_rdev, n + 1)
                nc.vector.tensor_tensor(xc[k % 2][:], xc[k % 2][:], spread(rdev, R), ALU.mult).then_inc(n_h, 1)

            def finish(k, c, i):
                dve.wait_ge(stored[k % 2], over(stored[k % 2], 16 * (2 * i + k // 2)))
                for h in range(2):
                    dve.wait_ge(pre_ready, over(pre_ready, 2 * c + h + 1))
                    half = slice(h * G, (h + 1) * G)
                    nc.vector.scalar_tensor_tensor(out=res[k % 2][:, half, :], in0=pre[k % 2][h][:].rearrange("p (r d) -> p r d", d=D),
                                                   scalar=0.0, in1=xs[k % NX][:, half, :], op0=ALU.max, op1=ALU.add).then_inc(res_ready, 1)

            centre(0, 0, 0)
            scale(0, 0, 0)

            def turn(k, n, i):
                centre(k, n, i)
                finish(k - 1, n - 1, i)
                scale(k, n, i)

            node_loop(dve, turn, 1)
            finish(NX, CHUNKS, CHUNKS // NX - 1)

        @block.scalar
        def _(act):
            act.wait_ge(ident_ready, 5)
            act.wait_ge(bias_loaded, 48)

            def edge_copies(k, b, t, last):
                act.wait_ge(g_centred, b + 1)
                nc.scalar.activation(sqg[:], hg[:], ACT.Square, scale=D ** -0.5).then_inc(g_squared, 1)
                act.wait_ge(g_var, b + 1)
                nc.scalar.activation(dev_g[:], var_g[:], ACT.Sqrt, bias=eps_t[:]).then_inc(g_dev, 1)
                act.wait_ge(e_turned, b + 1)
                nc.scalar.copy(eaT[:], pb[:, :]).then_inc(eaT_ready, 1)
                act.wait_ge(h_turned, over(h_turned, b + 1))
                nc.scalar.activation(hgT[:], pa[:, :], ACT.Relu).then_inc(hgT_ready, 1)
                act.wait_ge(g_msg, b + 1)
                nc.scalar.activation(msgT[:], pa[:, :], ACT.Relu, bias=msg_bias[:]).then_inc(msgT_ready, 1)
                act.wait_ge(g_update, b + 1)
                act.wait_ge(ys_stored[k], over(ys_stored[k], 16 * t))
                nc.scalar.copy(ys[k][:, :, 0:D], pb[:, :].rearrange("p (j d) -> p j d", d=D)).then_inc(ys_ready, 1)

            edge_loop(act, edge_copies)

            def square(k, n, i):
                act.wait_ge(n_centred, n + 1)
                act.wait_ge(n_var, over(n_var, n))
                nc.scalar.activation(sq[:], xc[k % 2][:], ACT.Square, scale=D ** -0.5).then_inc(n_squared, 1)

            def deviation(k, n, i):
                act.wait_ge(n_var, over(n_var, n + 1))
                nc.scalar.activation(dev[:], var[:], ACT.Sqrt, bias=eps_t[:]).then_inc(n_dev, 1)

            def relu(k, n, i):
                for h in range(2):
                    act.wait_ge(n_turned, over(n_turned, 2 * n + h + 1))
                    act.wait_ge(pre_ready, over(pre_ready, 2 * (n - 1)))
                    nc.scalar.activation(hT[k % 2][:, h, :], turned[h][:], ACT.Relu).then_inc(hT_ready, 1)

            def store(k, c):
                act.wait_ge(res_ready, over(res_ready, 2 * c + 2))
                act.dma_start(node_rows(out, HEAD + c * CHUNK), by_group(res[k % 2])).then_inc(stored[k % 2], 16)

            square(0, 0, 0)
            deviation(0, 0, 0)
            relu(0, 0, 0)

            def turn(k, n, i):
                square(k, n, i)
                store(k - 1, n - 1)
                deviation(k, n, i)
                relu(k, n, i)

            node_loop(act, turn, 1)
            act.wait_ge(res_ready, over(res_ready, 2 * CHUNKS + 2))
            act.dma_start(out[0:HEAD_G * GROUP, :].rearrange("(g p i) d -> p g (i d)", g=HEAD_G, i=2),
                          by_group(res[0])[:, 0:HEAD_G, :]).then_inc(stored[0], 16)
            act.dma_start(out[HEAD_G * GROUP:HEAD, :].rearrange("(p i) d -> p (i d)", i=2),
                          by_group(res[0])[:HEAD_P, HEAD_G, :]).then_inc(stored[0], 16)
            act.wait_ge(stored[0], over(stored[0], 16 * (CHUNKS // 2 + 2)))
            act.wait_ge(stored[1], over(stored[1], 16 * (CHUNKS // 2)))

        @block.tensor
        def _(pe):
            pe.wait_ge(ident_ready, 5)
            pe.wait_ge(weight_loaded, 16 * 8)
            for w in range(4):
                last = nc.tensor.transpose(pa[:, w * P:(w + 1) * P], weight_in[:, w, :], ident[:])
            last.then_inc(weight_turned, 1)
            pe.wait_ge(weight_ready, 1)

            def pair(tile, q):
                return tile[:, 2 * q:2 * q + 2, :].rearrange("p i d -> p (i d)")

            def edge_products(k, b, t, last):
                pe.wait_ge(edge_in[k], 48 * (t + 1))
                pe.wait_ge(ys_ready, over(ys_ready, b))
                for q in range(J // 2):
                    done = nc.tensor.transpose(pb[:, q * P:(q + 1) * P], pair(ea[k], q), ident[:])
                done.then_inc(e_turned, 1)
                pe.wait_ge(g_h, b + 1)
                pe.wait_ge(msgT_ready, over(msgT_ready, b))
                for q in range(J // 2):
                    done = nc.tensor.transpose(pa[:, q * P:(q + 1) * P], pair(hg, q), ident[:])
                done.then_inc(h_turned, 1)
                pe.wait_ge(eaT_ready, b + 1)
                pe.wait_ge(hgT_ready, b + 1)
                nc.tensor.matmul(pa[:, :], weight[:, MH, :], hgT[:], start=True, stop=False)
                nc.tensor.matmul(pa[:, :], weight[:, ME, :], eaT[:], start=False, stop=True).then_inc(g_msg, 1)
                pe.wait_ge(msgT_ready, over(msgT_ready, b + 1))
                for q in range(J // 2):
                    done = nc.tensor.matmul(pb[:, q * P:(q + 1) * P], msgT[:, q * P:(q + 1) * P], weight[:, UZ, :], start=True, stop=True)
                done.then_inc(g_update, 1)

            edge_loop(pe, edge_products)

            with pe.Fori(0, TILES) as t:
                pe.wait_ge(y_cols, t + 1)
                nc.tensor.transpose(pa[:, 0:P], dcol[:], ident[:]).then_inc(y_rows, 1)
                pe.wait_ge(y_same, t + 1)
                nc.tensor.matmul(pb[:, 0:D], same[:], yt[:, 0:D], start=True, stop=True).then_inc(y_sum, 1)

            def turn_rows(k, n, i):
                pe.wait_ge(n_h, n + 1)
                for h in range(2):
                    pe.wait_ge(hT_ready, over(hT_ready, 2 * n - 1 + h))
                    for q in range(G // 2):
                        done = nc.tensor.transpose(turned[h][:, q * P:(q + 1) * P], pair(xc[k % 2], h * G // 2 + q), ident[:])
                    done.then_inc(n_turned, 1)

            def products(k, n, i):
                pe.wait_ge(tab_loaded[k % 2], 16 * (2 * i + k // 2 + 1))
                for h in range(2):
                    pe.wait_ge(hT_ready, over(hT_ready, 2 * n + h + 1))
                    pe.wait_ge(res_ready, over(res_ready, 2 * n - 3 + h))
                    for q in range(G // 2):
                        bank_part = pre[k % 2][h][:, q * P:(q + 1) * P]
                        nc.tensor.matmul(bank_part, hT[k % 2][:, h, q * P:(q + 1) * P], weight[:, UH, :], start=True, stop=False)
                        done = nc.tensor.matmul(bank_part, ident[:], pair(tab[k % 2], h * G // 2 + q), start=False, stop=True)
                    done.then_inc(pre_ready, 1)

            def turn(k, n, i):
                turn_rows(k, n, i)
                products(k, n, i)

            turn(0, 0, 0)
            node_loop(pe, turn, 1)


_INS = ["x", "src", "dst", "edge_attr_64", "L0_gnn_M_W", "L0_gnn_M_b", "L0_gnn_U_W", "L0_gnn_U_b"]


def kernel(**inputs):
    import numpy as _np
    import concourse.bacc as _bacc
    from concourse.bass_utils import run_bass_kernel_spmd as _run

    nc = _bacc.Bacc("TRN2", target_bir_lowering=False, num_devices=1)
    arrays, args = {}, []
    for name in _INS:
        a = _np.ascontiguousarray(inputs[name])
        arrays[f"in_{name}"] = a
        args.append(nc.dram_tensor(f"in_{name}", a.shape, mybir.dt.from_np(a.dtype), kind="ExternalInput").ap())
    out = nc.dram_tensor("out_dram", inputs["x"].shape, F32, kind="ExternalOutput").ap()
    gnn_kernel(nc, *args, out)
    r = _run(nc, [arrays], core_ids=[0])
    return r.results[0]["out_dram"]
```

```python
import concourse.bass as bass
from concourse import mybir
from concourse.alu_op_type import AluOpType as ALU
from contextlib import ExitStack

F32 = mybir.dt.float32
I32 = mybir.dt.int32
ACT = mybir.ActivationFunctionType
AX = mybir.AxisListType

P = 128
D = 64
EPS = 1e-5


def gnn_kernel(nc, x, src, dst, edge_attr, M_W, M_b, U_W, U_b, out):
    N = x.shape[0]
    E = src.shape[0]

    G = 8
    GROUP = 2 * P
    CHUNK = G * GROUP
    CHUNKS = N // CHUNK
    HEAD = N - CHUNKS * CHUNK
    HEAD_G = HEAD // GROUP
    HEAD_P = (HEAD - HEAD_G * GROUP) // 2
    R = 2 * G
    HALF = R // 2 * D
    NX = 4
    PAIRS = CHUNKS // 2
    assert CHUNKS % NX == 0 and HEAD % 2 == 0

    J = 8
    BLOCK = P * J
    BLOCKS = -(-E // BLOCK)
    REST_P = (E - (BLOCKS - 1) * BLOCK) // J
    LAG = 3
    assert REST_P * J == E - (BLOCKS - 1) * BLOCK and BLOCKS % 2 == 1 and LAG % 2 == 1
    assert PAIRS - 1 + 2 == BLOCKS and (BLOCKS - LAG - 2) % 2 == 0

    HALF_AT, NODE_AT, YW = 2 * D, 2 * D + 1, 2 * D + 4
    WINDOW = 112
    TILES = -(-E // P)
    FAR = 1 << 20

    FINE = 200
    COARSE = E // FINE
    Q = (CHUNKS + 1) * G // 4
    assert COARSE * FINE == E and COARSE <= P and Q <= P

    ctx = ExitStack()
    with ctx:
        def sb(name, shape, dt=F32):
            return ctx.enter_context(nc.sbuf_tensor(name, shape, dt))

        given = []

        def sem(name, n=0):
            s = ctx.enter_context(nc.semaphore(name))
            if n:
                given.append((s, n))
            return s

        def over(s, n):
            return n + sum(g for t, g in given if t is s)

        messages = nc.dram_tensor("messages", [BLOCKS * BLOCK, YW], F32, kind="Internal").ap()
        table = nc.dram_tensor("table", [(CHUNKS + 1) * CHUNK, D], F32, kind="Internal").ap()
        first_dram = nc.dram_tensor("first_dram", [4 * Q], I32, kind="Internal").ap()

        column = sb("column", [P, P])
        row = sb("row", [P, 1])
        slot = sb("slot", [P, G, P])
        ident = sb("ident", [P, P])
        below = sb("below", [P, P])
        ones = sb("ones", [P, 1])
        eps_t = sb("eps_t", [P, 1])
        weight_in = sb("weight_in", [P, 4, P])
        weight = sb("weight", [P, 4, P])
        MH, ME, UH, UZ = range(4)
        msg_bias = sb("msg_bias", [P, 1])
        node_bias = sb("node_bias", [P, R * D])
        node_bias_row = sb("node_bias_row", [P, D])

        dst_rows = sb("dst_rows", [P, FINE], I32)
        dst_next = sb("dst_next", [P, FINE], I32)
        falls = sb("falls", [P, FINE])
        begin_i = sb("begin_i", [P, 5], I32)
        begin = sb("begin", [P, 5])
        allowed_i = sb("allowed_i", [P, 2], I32)
        allowed = sb("allowed", [P, 1])
        row_starts = sb("row_starts", [P, P])
        coarse_less = sb("coarse_less", [P, 5, COARSE])
        coarse = sb("coarse", [P, 5])
        coarse_i = sb("coarse_i", [P, 5], I32)
        fine = sb("fine", [P, 5, FINE], I32)
        fine_less = sb("fine_less", [P, 5, FINE])
        within = sb("within", [P, 5])
        first = sb("first", [P, 5])
        first_i = sb("first_i", [P, 4], I32)
        first_row = sb("first_row", [1, 4 * Q], I32)
        wide = sb("wide", [P, 4])
        unfit = sb("unfit", [P, 7])
        unfit_sum = sb("unfit_sum", [P, 1])
        general = sb("general", [1, 1], I32)

        xs = [sb(f"xs{k}", [P, R, D]) for k in range(NX)]
        win = [sb(f"win{k}", [P, G, YW]) for k in range(NX)]
        xc = [sb(f"xc{k}", [P, R, D]) for k in range(2)]
        sq = sb("sq", [P, R, D])
        total = sb("total", [P, R])
        var = sb("var", [P, R])
        dev = sb("dev", [P, R])
        rdev = [sb(f"rdev{k}", [P, R]) for k in range(2)]
        base = sb("base", [P, 1])
        hit = [sb(f"hit{k}", [P, G, P]) for k in range(2)]
        hT = [sb(f"hT{k}", [P, 2, HALF]) for k in range(2)]
        res = [sb(f"res{k}", [P, R, D]) for k in range(2)]

        src_all = sb("src_all", [P, BLOCKS, J], I32)
        dst_all = sb("dst_all", [P, BLOCKS, J], I32)
        half_i = sb("half_i", [P, BLOCKS, J], I32)
        odd_i = sb("odd_i", [P, BLOCKS, J], I32)
        number_all = sb("number_all", [P, BLOCKS, J, 2])
        side_all = sb("side_all", [P, BLOCKS, J, 2])
        src_i = [sb(f"src_i{k}", [P, J], I32) for k in range(2)]
        side = [sb(f"side{k}", [P, J, 2]) for k in range(2)]
        xg = [sb(f"xg{k}", [P, J, D]) for k in range(2)]
        ea = [sb(f"ea{k}", [P, J, D]) for k in range(2)]
        hg = sb("hg", [P, J, D])
        sqg = sb("sqg", [P, J, D])
        total_g = sb("total_g", [P, J])
        var_g = sb("var_g", [P, J])
        dev_g = sb("dev_g", [P, J])
        rdev_g = sb("rdev_g", [P, J])
        hgT = sb("hgT", [P, J * D])
        eaT = sb("eaT", [P, J * D])
        msgT = sb("msgT", [P, J * D])
        ys = [sb(f"ys{k}", [P, J, YW]) for k in range(2)]

        yt = sb("yt", [P, YW])
        dcol = sb("dcol", [P, P])
        same = sb("same", [P, P])
        earlier = sb("earlier", [P, P])
        n_before = sb("n_before", [P, 1])
        at_f = sb("at_f", [P, 1])
        read_i = sb("read_i", [P, 1], I32)
        write_i = sb("write_i", [P, 1], I32)
        t_old = sb("t_old", [P, D])
        t_half = sb("t_half", [P, D])
        t_new = sb("t_new", [P, D])

        bank = [ctx.enter_context(nc.psum_tensor(f"bank{k}", [P, 512], F32)) for k in range(8)]
        turned = bank[0:2]
        pre = [bank[2:4], bank[4:6]]
        pa, pb = bank[6], bank[7]

        went = sem("went")

        const_ready = sem("const_ready")
        ident_ready = sem("ident_ready")
        weight_cleared = sem("weight_cleared")
        weight_loaded = sem("weight_loaded")
        weight_turned = sem("weight_turned")
        weight_ready = sem("weight_ready")
        bias_loaded = sem("bias_loaded")
        bias_rows = sem("bias_rows")
        bias_ready = sem("bias_ready")
        table_filled = sem("table_filled")

        rows_loaded = sem("rows_loaded")
        plan_const = sem("plan_const")
        plan_step = sem("plan_step")
        plan_cols = sem("plan_cols")
        plan_turned = sem("plan_turned")
        coarse_ready = sem("coarse_ready")
        fine_loaded = sem("fine_loaded")
        first_ready = sem("first_ready")
        first_stored = sem("first_stored")
        first_loaded = sem("first_loaded")
        unfit_ready = sem("unfit_ready")
        unfit_counted = sem("unfit_counted")
        general_ready = sem("general_ready")

        index_cleared = sem("index_cleared")
        index_loaded = [sem(f"index_loaded{k}") for k in range(2)]
        index_ready = sem("index_ready")
        index_step = sem("index_step")
        src_ready = sem("src_ready")
        ea_loaded = [sem(f"ea_loaded{k}") for k in range(2)]
        gathered = [sem(f"gathered{k}") for k in range(2)]
        g_total = sem("g_total")
        g_centred = sem("g_centred")
        g_squared = sem("g_squared")
        g_side = sem("g_side")
        g_number = sem("g_number")
        g_var = sem("g_var")
        g_dev = sem("g_dev")
        g_rdev = sem("g_rdev")
        g_h = sem("g_h")
        e_turned = sem("e_turned")
        h_turned = sem("h_turned", 1)
        eaT_ready = sem("eaT_ready")
        hgT_ready = sem("hgT_ready")
        g_msg = sem("g_msg")
        msgT_ready = sem("msgT_ready", 1)
        g_update = sem("g_update")
        ys_ready = sem("ys_ready", 2)
        ys_stored = [sem(f"ys_stored{k}", 16) for k in range(2)]

        y_loaded = sem("y_loaded")
        y_cols = sem("y_cols")
        y_rows = sem("y_rows")
        y_same = sem("y_same")
        y_earlier = sem("y_earlier")
        y_before = sem("y_before")
        y_at = sem("y_at")
        y_read = sem("y_read")
        y_write = sem("y_write")
        y_sum = sem("y_sum")
        t_cleared = sem("t_cleared")
        t_read = sem("t_read")
        t_halfway = sem("t_halfway")
        t_summed = sem("t_summed")
        t_written = sem("t_written")

        x_loaded = [sem(f"x_loaded{k}") for k in range(NX)]
        win_loaded = [sem(f"win_loaded{k}") for k in range(NX)]
        n_total = sem("n_total")
        n_centred = sem("n_centred")
        n_squared = sem("n_squared")
        n_var = sem("n_var", 1)
        n_dev = sem("n_dev")
        n_rdev = sem("n_rdev")
        n_h = sem("n_h", 2)
        n_base = sem("n_base")
        hit_ready = sem("hit_ready")
        n_turned = sem("n_turned", 4)
        hT_ready = sem("hT_ready", 2)
        pre_ready = sem("pre_ready", 8)
        relu_ready = sem("relu_ready", 2)
        res_ready = [sem("res_ready0", 2), sem("res_ready1")]
        pre_read = [res_ready[0], relu_ready]
        stored = [sem(f"stored{k}", 16) for k in range(2)]

        def node_rows(t, begin):
            return t[bass.ds(begin, CHUNK), :].rearrange("(g p i) d -> p g (i d)", g=G, i=2)

        def by_group(tile):
            return tile[:].rearrange("p (g i) d -> p g (i d)", i=2)

        def spread(stat, n):
            return stat[:].unsqueeze(2).to_broadcast([P, n, D])

        def pair_of(tile, q):
            return tile[:, 2 * q:2 * q + 2, :].rearrange("p i d -> p (i d)")

        def edges(i, m):
            return 2 * i + m, m % 2, i + m // 2

        def chunk(i, m):
            return NX * i + m, m

        def turns(i, m):
            return i + m // NX

        def before(i, m):
            return 2 * i + m // 2

        def chunk_begin(i, m):
            return 0 if isinstance(i, int) and NX * i + m == CHUNKS else HEAD + (NX * i + m) * CHUNK

        def wait_alone(engine, s, value):
            engine.wait_ge(s, value)
            engine.sem_inc(went, 1)

        def both_ways(engine, fast, slow):
            engine.wait_ge(general_ready, 1)
            unfits = engine.value_load(general[0:1, 0:1], min_val=0, max_val=1)
            with engine.If(unfits == 0):
                fast()
            with engine.Else():
                slow()

        def blocks_alone(engine, step):
            with engine.Fori(0, (BLOCKS - LAG) // 2) as i:
                for k in range(2):
                    step(*edges(i, LAG + k))

        def pairs(engine, pair, windows):
            def block_of(i, m):
                there = windows and not (isinstance(i, int) and LAG + 2 * i + m // 2 >= BLOCKS)
                return edges(i, LAG + m // 2) if there else None
            pair(0, 0, block_of(0, 0), None, windows)
            loops = (BLOCKS - LAG - 1) // 2
            with engine.Fori(0, loops) as i:
                for m in (2, 4):
                    pair(i, m, block_of(i, m), block_of(i, m - 2), windows)
            for j in range(2 * loops + 1, PAIRS):
                pair(0, 2 * j, block_of(0, 2 * j), block_of(0, 2 * j - 2), windows)
            pair(0, CHUNKS, None, None, windows)

        block = ctx.enter_context(nc.Block())

        @block.sync
        def _(sp):
            for s, n in given:
                sp.sem_inc(s, n)

            def by_edge(dram, b, n, m=P):
                return dram[b * BLOCK:b * BLOCK + n * m * J].rearrange("(b p j) -> p b j", p=m, j=J)

            def load_edges(b, k, t, n=P):
                if t is not None:
                    wait_alone(sp, e_turned, b - 1)
                sp.dma_start(ea[k][:n, :, :], edge_attr[bass.ds(b * BLOCK, n * J), :].rearrange("(p j) d -> p j d", j=J)).then_inc(ea_loaded[k], 16)

            sp.wait_ge(index_cleared, 2)
            for k, (b, n) in enumerate([(0, LAG), (LAG, BLOCKS - 1 - LAG)]):
                for dram, tile in ((src, src_all), (dst, dst_all)):
                    sp.dma_start(tile[:, b:b + n, :], by_edge(dram, b, n)).then_inc(index_loaded[k], 16)
                if k == 0:
                    load_edges(0, 0, None)
                    load_edges(1, 1, None)
            for dram, tile in ((src, src_all), (dst, dst_all)):
                sp.dma_start(tile[:REST_P, BLOCKS - 1:BLOCKS, :], by_edge(dram, BLOCKS - 1, 1, REST_P)).then_inc(index_loaded[1], 16)
            sp.wait_ge(weight_cleared, 1)
            for w, (m, at) in enumerate([(M_W, 0), (M_W, D), (U_W, 0), (U_W, D)]):
                for h in (0, D):
                    sp.dma_start(weight_in[h:h + D, w, h:h + D], m[:, at:at + D]).then_inc(weight_loaded, 16)
            for h in (0, D):
                sp.dma_start(msg_bias[h:h + D, :], M_b.rearrange("(p a) -> p a", a=1)).then_inc(bias_loaded, 16)
            sp.dma_start(node_bias_row[:], U_b.rearrange("(a d) -> a d", a=1).to_broadcast([P, D])).then_inc(bias_loaded, 16)
            sp.dma_start(dst_rows[:COARSE, :], dst.rearrange("(r c) -> r c", c=FINE)).then_inc(rows_loaded, 16)
            sp.dma_start(dst_next[:COARSE - 1, :], dst[1:1 + (COARSE - 1) * FINE].rearrange("(r c) -> r c", c=FINE)).then_inc(rows_loaded, 16)
            sp.dma_start(dst_next[COARSE - 1:COARSE, 0:FINE - 1], dst[1 + (COARSE - 1) * FINE:E].rearrange("(r c) -> r c", r=1)).then_inc(rows_loaded, 16)
            for n in range(NX):
                sp.dma_start(by_group(xs[n]), node_rows(x, HEAD + n * CHUNK)).then_inc(x_loaded[n], 16)
            for k in range(NX):
                for h in (0, D):
                    sp.dma_start(win[k][WINDOW:WINDOW + 1, :, h:h + D],
                                 U_b.rearrange("(a b d) -> a b d", a=1, b=1).to_broadcast([1, G, D])).then_inc(bias_rows, 16)
            load_edges(2, 0, 1)
            load_edges(3, 1, 1)
            load_edges(4, 0, 2)
            sp.wait_ge(first_ready, 1)
            sp.dma_start(first_dram.rearrange("(q s) -> q s", s=4), first_i[:Q, :]).then_inc(first_stored, 16)
            sp.wait_ge(first_stored, 16)
            sp.dma_start(first_row[:], first_dram.rearrange("(a q) -> a q", a=1)).then_inc(first_loaded, 16)
            sp.wait_ge(first_loaded, 16)

            def load_windows(i, m):
                n, _ = chunk(i, m)
                if isinstance(i, int) and n == CHUNKS:
                    slots = (BLOCKS // 2 + 1, BLOCKS // 2)
                else:
                    slots = i + (m // 2 + 1) // 2 + 1, i + (m // 2 + 2) // 2
                for k in range(2):
                    wait_alone(sp, ys_stored[k], over(ys_stored[k], 16 * slots[k]))
                wait_alone(sp, pre_ready, over(pre_ready, 2 * (n - 3)))
                _, starts = nc.values_load_multi_w_load_instructions(first_row[0:1, bass.ds(n * G, G)], engines=[sp.engine], min_val=0, max_val=E)
                for g in range(G):
                    sp.dma_start(win[m % NX][:WINDOW, g, :], messages[bass.ds(starts[g], WINDOW), :]).then_inc(win_loaded[m % NX], 16)

            def fast():
                def edges_and_windows(i, m, next_block, last):
                    if next_block:
                        b, k, t = next_block
                        load_edges(b, k, t, REST_P if last else P)
                    load_windows(i, m)
                    load_windows(i, m + 1)
                sp.wait_ge(bias_rows, 16 * 2 * NX)
                loops = (BLOCKS - 1 - LAG - 2) // 2 - 1
                edges_and_windows(0, 0, None, False)
                with sp.Fori(0, loops) as i:
                    for m in (2, 4):
                        edges_and_windows(i, m, edges(i, LAG + 1 + m // 2), False)
                for j in range(2 * loops + 1, PAIRS):
                    b = LAG + 1 + j
                    edges_and_windows(0, 2 * j, edges(0, b) if b < BLOCKS else None, b == BLOCKS - 1)
                load_windows(0, CHUNKS)

            def slow():
                with sp.Fori(0, (BLOCKS - LAG - 3) // 2 ) as i:
                    for k in range(2):
                        load_edges(*edges(i, LAG + 2 + k))
                for b in range(LAG + 2 + 2 * ((BLOCKS - LAG - 3) // 2), BLOCKS):
                    load_edges(*edges(0, b), REST_P if b == BLOCKS - 1 else P)
                sp.wait_ge(bias_ready, 1)
                for c in range(CHUNKS + 1):
                    sp.dma_start(table[c * CHUNK:(c + 1) * CHUNK, :].rearrange("(p r) d -> p (r d)", p=P), node_bias[:]).then_inc(table_filled, 16)
                sp.wait_ge(ys_stored[0], over(ys_stored[0], 16 * (BLOCKS // 2 + 1)))
                sp.wait_ge(ys_stored[1], over(ys_stored[1], 16 * (BLOCKS // 2)))
                sp.wait_ge(table_filled, 16 * (CHUNKS + 1))
                sp.dma_start(yt[:], messages[0:P, :]).then_inc(y_loaded, 16)
                with sp.Fori(1, TILES) as t:
                    wait_alone(sp, t_written, 16 * t)
                    sp.dma_start(yt[:], messages[bass.ds(t * P, P), :]).then_inc(y_loaded, 16)
                sp.wait_ge(t_written, 16 * TILES)
                sp.wait_ge(bias_rows, 16 * 2 * NX)

                def load_table(i, m):
                    n, _ = chunk(i, m)
                    wait_alone(sp, pre_ready, over(pre_ready, 2 * (n - 3)))
                    sp.dma_start(win[m % NX][:, :, 0:2 * D], node_rows(table, chunk_begin(i, m))).then_inc(win_loaded[m % NX], 16)

                with sp.Fori(0, CHUNKS // NX) as i:
                    for m in range(NX):
                        load_table(i, m)
                load_table(0, CHUNKS)

            both_ways(sp, fast, slow)

        @block.gpsimd
        def _(pool):
            nc.gpsimd.memset(src_all[:], 0).then_inc(index_cleared, 1)
            nc.gpsimd.memset(dst_all[:], FAR).then_inc(index_cleared, 1)
            nc.gpsimd.memset(weight_in[:], 0.0).then_inc(weight_cleared, 1)
            nc.gpsimd.iota(column[:], pattern=[[1, P]], base=0, channel_multiplier=0, allow_small_or_imprecise_dtypes=True).then_inc(const_ready, 1)
            nc.gpsimd.iota(row[:], pattern=[[0, 1]], base=0, channel_multiplier=1, allow_small_or_imprecise_dtypes=True).then_inc(const_ready, 1)
            nc.gpsimd.iota(begin_i[:], pattern=[[GROUP, 5]], base=HEAD, channel_multiplier=4 * GROUP).then_inc(plan_const, 1)
            nc.gpsimd.iota(allowed_i[:], pattern=[[0, 2]], base=0, channel_multiplier=1).then_inc(plan_const, 1)

            def gather_begin(b, k, t, used=True):
                if used:
                    wait_alone(pool, gathered[k], 16 * J * t)
                nc.gpsimd.tensor_copy(src_i[k][:], src_all[:, b, :] if isinstance(b, int) else src_all[:, bass.ds(b, 1), :].rearrange("p b j -> p (b j)")).then_inc(src_ready, 1)
                if used:
                    wait_alone(pool, g_centred, b - 1)
                wait_alone(pool, src_ready, b + 1)

            def gather_rows(b, k, t, columns=range(J)):
                for j in columns:
                    pool.indirect_dma_start(out=xg[k][:, j, :], out_offset=None, in_=x[:, :],
                                            in_offset=bass.IndirectOffsetOnAxis(ap=src_i[k][:, j:j + 1], axis=0)).then_inc(gathered[k], 16)

            def gather(b, k, t, used=True):
                gather_begin(b, k, t, used)
                gather_rows(b, k, t)

            pool.wait_ge(index_loaded[0], 32)
            gather(*edges(0, 0), False)
            nc.gpsimd.iota(slot[:], pattern=[[P, G], [1, P]], base=0, channel_multiplier=0, allow_small_or_imprecise_dtypes=True).then_inc(const_ready, 1)
            gather(*edges(0, 1), False)
            pool.wait_ge(coarse_ready, 1)
            for s in range(5):
                pool.indirect_dma_start(out=fine[:Q, s, :], out_offset=None, in_=dst.rearrange("(r c) -> r c", c=FINE),
                                        in_offset=bass.IndirectOffsetOnAxis(ap=coarse_i[:Q, s:s + 1], axis=0)).then_inc(fine_loaded, 16)
            gather(*edges(0, 2))
            pool.wait_ge(index_loaded[1], 64)
            gather(*edges(0, LAG))

            def scale(i, m):
                n, _ = chunk(i, m)
                pool.wait_ge(n_rdev, n + 1)
                nc.gpsimd.tensor_tensor(xc[m % 2][:], xc[m % 2][:], spread(rdev[m % 2], R), ALU.mult).then_inc(n_h, 1)

            def add_rows(i, m):
                for h in range(2):
                    half = slice(h * G, (h + 1) * G)
                    pool.wait_ge(relu_ready, over(relu_ready, 2 * before(i, m) + h + 1))
                    nc.gpsimd.tensor_tensor(res[m % 2][:, half, :], res[m % 2][:, half, :], xs[m % NX][:, half, :], ALU.add).then_inc(res_ready[1], 1)

            def pair(i, m, b, prev, windows):
                begins, ends = isinstance(i, int) and m == 0, isinstance(i, int) and m == CHUNKS
                gathers = b and not (isinstance(i, int) and b[0] == BLOCKS - 1)
                if gathers:
                    later = edges(i, LAG + 1 + m // 2)
                    gather_begin(*later)
                    gather_rows(*later, range(J // 2))
                scale(i, m)
                if gathers:
                    gather_rows(*later, range(J // 2, J))
                if not begins:
                    add_rows(i, m - 1)
                if not ends:
                    scale(i, m + 1)

            def slow():
                alone = BLOCKS - LAG - 1
                with pool.Fori(0, alone // 2) as i:
                    for k in range(2):
                        gather(*edges(i, LAG + 1 + k))
                gather(*edges(0, BLOCKS - 1))
                nc.gpsimd.memset(t_old[:], 0.0).then_inc(t_cleared, 1)
                pool.wait_ge(t_cleared, 1)
                with pool.Fori(0, TILES) as t:
                    wait_alone(pool, y_read, t + 1)
                    pool.indirect_dma_start(out=t_old[:], out_offset=None, in_=table[:, :],
                                            in_offset=bass.IndirectOffsetOnAxis(ap=read_i[:], axis=0),
                                            bounds_check=N - 1, oob_is_err=False).then_inc(t_read, 16)
                    wait_alone(pool, t_summed, t + 1)
                    wait_alone(pool, y_write, t + 1)
                    pool.indirect_dma_start(out=table[:, :], out_offset=bass.IndirectOffsetOnAxis(ap=write_i[:], axis=0),
                                            in_=t_new[:], in_offset=None,
                                            bounds_check=N - 1, oob_is_err=False).then_inc(t_written, 16)
                pairs(pool, pair, False)

            both_ways(pool, lambda: pairs(pool, pair, True), slow)

        @block.vector
        def _(dve):
            dve.wait_ge(const_ready, 2)
            nc.vector.tensor_scalar(ident[:], column[:], row[:], None, ALU.is_equal).then_inc(ident_ready, 1)
            nc.vector.memset(eps_t[:], EPS).then_inc(ident_ready, 1)
            nc.vector.memset(ones[:], 1.0).then_inc(ident_ready, 1)
            nc.vector.tensor_scalar(below[:], column[:], row[:], None, ALU.is_lt).then_inc(ident_ready, 1)
            for k in range(2):
                nc.vector.memset(hit[k][:], 1.0).then_inc(ident_ready, 1)
                nc.vector.memset(ys[k][:], 0.0).then_inc(ident_ready, 1)
            nc.vector.memset(base[:], float(HEAD // 2)).then_inc(n_base, 1)
            nc.vector.memset(unfit[:], 0.0).then_inc(ident_ready, 1)
            dve.wait_ge(ident_ready, 9)

            steps = []

            def step(instruction):
                steps.append(instruction.then_inc(plan_step, 1))
                dve.wait_ge(plan_step, len(steps))

            def number_blocks(b, n):
                part = slice(b, b + n)
                step(nc.vector.tensor_single_scalar(half_i[:, part, :], dst_all[:, part, :], 1, ALU.logical_shift_right))
                step(nc.vector.tensor_single_scalar(odd_i[:, part, :], dst_all[:, part, :], 1, ALU.bitwise_and))
                step(nc.vector.tensor_copy(number_all[:, part, :, 0:1], half_i[:, part, :].unsqueeze(3)))
                step(nc.vector.tensor_copy(number_all[:, part, :, 1:2], dst_all[:, part, :].unsqueeze(3)))
                step(nc.vector.tensor_scalar(side_all[:, part, :, 0:1], odd_i[:, part, :].unsqueeze(3), -1.0, 1.0, ALU.mult, ALU.add))
                step(nc.vector.tensor_copy(side_all[:, part, :, 1:2], odd_i[:, part, :].unsqueeze(3)))

            def edge_centre(b, k, t):
                dve.wait_ge(gathered[k], 16 * J * (t + 1))
                nc.vector.tensor_reduce(total_g[:], xg[k][:], AX.X, ALU.add).then_inc(g_total, 1)
                dve.wait_ge(ys_stored[k], over(ys_stored[k], 16 * t))
                nc.vector.tensor_copy(ys[k][:, :, HALF_AT:NODE_AT + 1], number_all[:, bass.ds(b, 1), :, :].rearrange("p b j c -> p (b j) c")).then_inc(g_number, 1)
                nc.vector.tensor_copy(side[k][:], side_all[:, bass.ds(b, 1), :, :].rearrange("p b j c -> p (b j) c")).then_inc(g_side, 1)
                dve.wait_ge(g_total, b + 1)
                dve.wait_ge(h_turned, over(h_turned, b))
                nc.vector.scalar_tensor_tensor(out=hg[:], in0=spread(total_g, J), scalar=-1.0 / D, in1=xg[k][:],
                                               op0=ALU.mult, op1=ALU.add).then_inc(g_centred, 1)

            def edge_variance(b, k, t):
                dve.wait_ge(g_squared, b + 1)
                nc.vector.tensor_reduce(var_g[:], sqg[:], AX.X, ALU.add).then_inc(g_var, 1)

            def edge_scale(b, k, t):
                dve.wait_ge(g_dev, b + 1)
                nc.vector.reciprocal(rdev_g[:], dev_g[:]).then_inc(g_rdev, 1)
                dve.wait_ge(g_rdev, b + 1)
                nc.vector.tensor_tensor(hg[:], hg[:], spread(rdev_g, J), ALU.mult).then_inc(g_h, 1)

            def edge_norm(b, k, t):
                edge_centre(b, k, t)
                edge_variance(b, k, t)
                edge_scale(b, k, t)

            def plan():
                dve.wait_ge(rows_loaded, 48)
                dve.wait_ge(plan_const, 2)
                nc.vector.tensor_copy(dcol[:COARSE, :], dst_rows[:COARSE, 0:1].to_broadcast([COARSE, P])).then_inc(plan_cols, 1)
                step(nc.vector.tensor_copy(begin[:], begin_i[:]))
                odd_q = Q - G // 4
                step(nc.vector.tensor_scalar(allowed[:], row[:], float(odd_q), -float(N), ALU.is_ge, ALU.mult))
                step(nc.vector.tensor_scalar(begin[:], begin[:], allowed[:], None, ALU.add))
                step(nc.vector.tensor_single_scalar(allowed_i[:], allowed_i[:], 2, ALU.logical_shift_right))
                step(nc.vector.tensor_copy(allowed[:], allowed_i[:, 0:1]))
                step(nc.vector.tensor_scalar(allowed[:], allowed[:], float(BLOCK), float(2 * BLOCK - WINDOW), ALU.mult, ALU.add))
                dve.wait_ge(plan_turned, 1)
                step(nc.vector.tensor_copy(row_starts[:, 0:COARSE], pb[:, 0:COARSE]))
                step(nc.vector.tensor_tensor(coarse_less[:], row_starts[:, 0:COARSE].unsqueeze(1).to_broadcast([P, 5, COARSE]),
                                             begin[:].unsqueeze(2).to_broadcast([P, 5, COARSE]), ALU.is_lt))
                step(nc.vector.tensor_reduce(coarse[:], coarse_less[:], AX.X, ALU.add))
                step(nc.vector.tensor_scalar(coarse[:], coarse[:], -1.0, 0.0, ALU.add, ALU.max))
                nc.vector.tensor_copy(coarse_i[:], coarse[:]).then_inc(coarse_ready, 1)

            def plan_end():
                step(nc.vector.tensor_tensor(falls[:COARSE, 0:FINE - 1], dst_rows[:COARSE, 0:FINE - 1], dst_next[:COARSE, 0:FINE - 1], ALU.is_gt))
                step(nc.vector.tensor_reduce(unfit[:COARSE, 0:1], falls[:COARSE, 0:FINE - 1], AX.X, ALU.max))
                step(nc.vector.tensor_tensor(falls[:COARSE - 1, FINE - 1:FINE], dst_rows[:COARSE - 1, FINE - 1:FINE], dst_next[:COARSE - 1, FINE - 1:FINE], ALU.is_gt))
                step(nc.vector.tensor_tensor(unfit[:COARSE - 1, 0:1], unfit[:COARSE - 1, 0:1], falls[:COARSE - 1, FINE - 1:FINE], ALU.max))
                dve.wait_ge(fine_loaded, 16 * 5)
                step(nc.vector.tensor_tensor(fine_less[:Q], fine[:Q], begin[:Q].unsqueeze(2).to_broadcast([Q, 5, FINE]), ALU.is_lt))
                step(nc.vector.tensor_reduce(within[:Q], fine_less[:Q], AX.X, ALU.add))
                step(nc.vector.scalar_tensor_tensor(out=first[:Q], in0=coarse[:Q], scalar=float(FINE), in1=within[:Q], op0=ALU.mult, op1=ALU.add))
                nc.vector.tensor_copy(first_i[:Q], first[:Q, 0:4]).then_inc(first_ready, 1)
                step(nc.vector.tensor_scalar(unfit[:Q, 1:2], first[:Q, 3:4], allowed[:Q], None, ALU.is_gt))
                step(nc.vector.tensor_tensor(wide[:Q], first[:Q, 1:5], first[:Q, 0:4], ALU.subtract))
                step(nc.vector.tensor_scalar(unfit[:Q, 2:6], wide[:Q], float(WINDOW), None, ALU.is_gt))
                nc.vector.tensor_reduce(unfit_sum[:], unfit[:, 0:6], AX.X, ALU.max).then_inc(unfit_ready, 1)
                dve.wait_ge(unfit_counted, 1)
                nc.vector.tensor_scalar(general[:], pb[0:1, 0:1], 1.0, None, ALU.min).then_inc(general_ready, 1)

            dve.wait_ge(index_loaded[0], 32)
            number_blocks(0, LAG)
            dve.wait_ge(weight_turned, 1)
            nc.vector.tensor_copy(weight[:].rearrange("p w c -> p (w c)"), pa[:, :]).then_inc(weight_ready, 1)
            plan()
            edge_norm(*edges(0, 0))
            edge_norm(*edges(0, 1))
            plan_end()
            dve.wait_ge(index_loaded[1], 64)
            number_blocks(LAG, BLOCKS - LAG)
            dve.wait_ge(bias_loaded, 48)
            nc.vector.tensor_copy(node_bias[:].rearrange("p (r d) -> p r d", d=D),
                                  node_bias_row[:].unsqueeze(1).to_broadcast([P, R, D])).then_inc(bias_ready, 1)
            dve.wait_ge(const_ready, 3)
            edge_norm(*edges(0, 2))

            def centre(i, m):
                n, _ = chunk(i, m)
                dve.wait_ge(x_loaded[m % NX], 16 * (turns(i, m) + 1))
                nc.vector.tensor_reduce(total[:], xs[m % NX][:], AX.X, ALU.add).then_inc(n_total, 1)
                dve.wait_ge(n_total, n + 1)
                dve.wait_ge(n_turned, over(n_turned, 2 * n - 2))
                nc.vector.scalar_tensor_tensor(out=xc[m % 2][:], in0=spread(total, R), scalar=-1.0 / D, in1=xs[m % NX][:],
                                               op0=ALU.mult, op1=ALU.add).then_inc(n_centred, 1)

            def find_hits(i, m):
                n, _ = chunk(i, m)
                odd = isinstance(i, int) and n == CHUNKS
                dve.wait_ge(win_loaded[m % NX], 16 * G * (turns(i, m) + 1))
                dve.wait_ge(pre_ready, over(pre_ready, 2 * n - 2))
                dve.wait_ge(n_base, n + 1)
                nc.vector.scalar_tensor_tensor(out=hit[m % 2][:WINDOW], in0=slot[:WINDOW], scalar=0.0 if odd else base[:WINDOW, 0:1],
                                               in1=win[m % NX][:WINDOW, :, HALF_AT:HALF_AT + 1].to_broadcast([WINDOW, G, P]),
                                               op0=ALU.add, op1=ALU.is_equal).then_inc(hit_ready, 1)
                if not odd:
                    dve.wait_ge(hit_ready, n + 1)
                    nc.vector.tensor_scalar(base[:], base[:], float(CHUNK // 2), None, ALU.add).then_inc(n_base, 1)

            def variance(i, m):
                n, _ = chunk(i, m)
                dve.wait_ge(n_squared, n + 1)
                nc.vector.tensor_reduce(var[:], sq[:], AX.X, ALU.add).then_inc(n_var, 1)

            def inverse(i, m):
                n, _ = chunk(i, m)
                dve.wait_ge(n_dev, n + 1)
                dve.wait_ge(n_h, over(n_h, n - 1))
                nc.vector.reciprocal(rdev[m % 2][:], dev[:]).then_inc(n_rdev, 1)

            def finish(i, m):
                n, _ = chunk(i, m)
                dve.wait_ge(stored[0], over(stored[0], 16 * before(i, m)))
                for h in range(2):
                    dve.wait_ge(pre_ready, over(pre_ready, 2 * n + h + 1))
                    half = slice(h * G, (h + 1) * G)
                    nc.vector.scalar_tensor_tensor(out=res[0][:, half, :], in0=pre[0][h][:].rearrange("p (r d) -> p r d", d=D),
                                                   scalar=0.0, in1=xs[m % NX][:, half, :], op0=ALU.max, op1=ALU.add).then_inc(res_ready[0], 1)

            def pair(i, m, b, prev, windows):
                begins, ends = isinstance(i, int) and m == 0, isinstance(i, int) and m == CHUNKS
                centre(i, m)
                if b:
                    edge_centre(*b)
                if windows and not begins:
                    find_hits(i, m - 1)
                variance(i, m)
                if b:
                    edge_variance(*b)
                inverse(i, m)
                if not begins:
                    finish(i, m - 2)
                if not ends:
                    centre(i, m + 1)
                if b:
                    edge_scale(*b)
                if not ends:
                    variance(i, m + 1)
                if windows:
                    find_hits(i, m)
                if not ends:
                    inverse(i, m + 1)
                else:
                    finish(i, m)

            def slow():
                blocks_alone(dve, edge_norm)
                with dve.Fori(0, TILES) as t:
                    dve.wait_ge(y_loaded, 16 * t + 16)
                    nc.vector.tensor_copy(dcol[:], yt[:, NODE_AT:NODE_AT + 1].to_broadcast([P, P])).then_inc(y_cols, 1)
                    nc.vector.tensor_copy(read_i[:], yt[:, NODE_AT:NODE_AT + 1]).then_inc(y_read, 1)
                    dve.wait_ge(y_rows, t + 1)
                    nc.vector.tensor_scalar(same[:], pa[:, 0:P], yt[:, NODE_AT:NODE_AT + 1], None, ALU.is_equal).then_inc(y_same, 1)
                    dve.wait_ge(y_same, t + 1)
                    nc.vector.tensor_tensor(earlier[:], same[:], below[:], ALU.mult).then_inc(y_earlier, 1)
                    dve.wait_ge(y_earlier, t + 1)
                    nc.vector.tensor_reduce(n_before[:], earlier[:], AX.X, ALU.add).then_inc(y_before, 1)
                    dve.wait_ge(y_before, t + 1)
                    nc.vector.tensor_scalar(at_f[:], n_before[:], 0.0, float(FAR), ALU.is_gt, ALU.mult).then_inc(y_at, 1)
                    dve.wait_ge(y_at, t + 1)
                    nc.vector.tensor_tensor(write_i[:], at_f[:], yt[:, NODE_AT:NODE_AT + 1], ALU.add).then_inc(y_write, 1)
                    dve.wait_ge(y_sum, t + 1)
                    dve.wait_ge(t_read, 16 * t + 16)
                    nc.vector.tensor_tensor(t_half[:], pb[:, 0:D], t_old[:], ALU.add).then_inc(t_halfway, 1)
                    dve.wait_ge(t_halfway, t + 1)
                    nc.vector.tensor_tensor(t_new[:], pb[:, D:2 * D], t_half[:], ALU.add).then_inc(t_summed, 1)
                pairs(dve, pair, False)

            both_ways(dve, lambda: pairs(dve, pair, True), slow)

        @block.scalar
        def _(act):
            act.wait_ge(ident_ready, 9)
            act.wait_ge(bias_loaded, 48)

            def edge_square(b, k, t):
                act.wait_ge(g_centred, b + 1)
                nc.scalar.activation(sqg[:], hg[:], ACT.Square, scale=D ** -0.5).then_inc(g_squared, 1)

            def edge_features(b, k, t):
                act.wait_ge(e_turned, b + 1)
                nc.scalar.copy(eaT[:], pa[:, :]).then_inc(eaT_ready, 1)

            def edge_deviation(b, k, t):
                act.wait_ge(g_var, b + 1)
                nc.scalar.activation(dev_g[:], var_g[:], ACT.Sqrt, bias=eps_t[:]).then_inc(g_dev, 1)

            def edge_relu(b, k, t):
                act.wait_ge(h_turned, over(h_turned, b + 1))
                nc.scalar.activation(hgT[:], pa[:, :], ACT.Relu).then_inc(hgT_ready, 1)

            def edge_message(b, k, t):
                act.wait_ge(g_msg, b + 1)
                nc.scalar.activation(msgT[:], pa[:, :], ACT.Relu, bias=msg_bias[:]).then_inc(msgT_ready, 1)

            def edge_rows(b, k, t, s):
                if s == 0:
                    act.wait_ge(g_update, b + 1)
                    act.wait_ge(g_side, b + 1)
                    act.wait_ge(ys_stored[k], over(ys_stored[k], 16 * t))
                for j in range(J):
                    done = nc.scalar.activation(ys[k][:, j, s * D:(s + 1) * D], pb[:, j * D:(j + 1) * D], ACT.Identity, scale=side[k][:, j, s:s + 1])
                done.then_inc(ys_ready, 1)

            def edge_store(b, k, t):
                act.wait_ge(ys_ready, over(ys_ready, 2 * b + 2))
                act.wait_ge(g_number, b + 1)
                act.dma_start(messages[bass.ds(b * BLOCK, BLOCK), :].rearrange("(p j) d -> p j d", j=J), ys[k][:]).then_inc(ys_stored[k], 16)

            def edge_copies(b, k, t):
                for part in (edge_features, edge_square, edge_deviation, edge_relu, edge_message):
                    part(b, k, t)
                for s in range(2):
                    edge_rows(b, k, t, s)
                edge_store(b, k, t)

            for b in range(LAG):
                edge_copies(*edges(0, b))

            def square(i, m):
                n, _ = chunk(i, m)
                act.wait_ge(n_centred, n + 1)
                act.wait_ge(n_var, over(n_var, n))
                nc.scalar.activation(sq[:], xc[m % 2][:], ACT.Square, scale=D ** -0.5).then_inc(n_squared, 1)

            def deviation(i, m):
                n, _ = chunk(i, m)
                act.wait_ge(n_var, over(n_var, n + 1))
                nc.scalar.activation(dev[:], var[:], ACT.Sqrt, bias=eps_t[:]).then_inc(n_dev, 1)

            def relu(i, m):
                n, _ = chunk(i, m)
                act.wait_ge(pre_ready, over(pre_ready, 2 * (n - 1)))
                for h in range(2):
                    act.wait_ge(n_turned, over(n_turned, 2 * n + h + 1))
                    nc.scalar.activation(hT[m % 2][:, h, :], turned[h][:], ACT.Relu).then_inc(hT_ready, 1)

            def last_relu(i, m):
                n, _ = chunk(i, m)
                act.wait_ge(stored[1], over(stored[1], 16 * before(i, m)))
                for h in range(2):
                    act.wait_ge(pre_ready, over(pre_ready, 2 * n + h + 1))
                    nc.scalar.activation(res[1][:, h * G:(h + 1) * G, :], pre[1][h][:].rearrange("p (r d) -> p r d", d=D), ACT.Relu).then_inc(relu_ready, 1)

            def store(i, m):
                n, _ = chunk(i, m)
                act.wait_ge(res_ready[m % 2], over(res_ready[m % 2], 2 * before(i, m) + 2))
                act.dma_start(node_rows(out, chunk_begin(i, m)), by_group(res[m % 2])).then_inc(stored[m % 2], 16)
                if not (isinstance(i, int) and n + NX > CHUNKS):
                    act.dma_start(by_group(xs[m % NX]), node_rows(x, chunk_begin(i, m + NX))).then_inc(x_loaded[m % NX], 16)

            def pair(i, m, b, prev, windows):
                begins, ends = isinstance(i, int) and m == 0, isinstance(i, int) and m == CHUNKS
                square(i, m)
                if b:
                    edge_square(*b)
                if prev:
                    edge_rows(*prev, 0)
                deviation(i, m)
                if b:
                    edge_deviation(*b)
                if not begins:
                    relu(i, m - 1)
                    store(i, m - 2)
                if prev:
                    edge_rows(*prev, 1)
                if b:
                    edge_features(*b)
                if not ends:
                    square(i, m + 1)
                if not begins:
                    last_relu(i, m - 1)
                if b:
                    edge_relu(*b)
                if not ends:
                    deviation(i, m + 1)
                if prev:
                    edge_store(*prev)
                relu(i, m)
                if b:
                    edge_message(*b)
                if not begins:
                    store(i, m - 1)

            def store_odd():
                act.wait_ge(res_ready[0], over(res_ready[0], 2 * (CHUNKS // 2) + 2))
                act.dma_start(out[0:HEAD_G * GROUP, :].rearrange("(g p i) d -> p g (i d)", g=HEAD_G, i=2),
                              by_group(res[0])[:, 0:HEAD_G, :]).then_inc(stored[0], 16)
                act.dma_start(out[HEAD_G * GROUP:HEAD, :].rearrange("(p i) d -> p (i d)", i=2),
                              by_group(res[0])[:HEAD_P, HEAD_G, :]).then_inc(stored[0], 16)
                act.wait_ge(stored[0], over(stored[0], 16 * (CHUNKS // 2 + 2)))
                act.wait_ge(stored[1], over(stored[1], 16 * (CHUNKS // 2)))

            def fast():
                pairs(act, pair, True)
                store_odd()

            def slow():
                blocks_alone(act, edge_copies)
                pairs(act, pair, False)
                store_odd()

            both_ways(act, fast, slow)

        @block.tensor
        def _(pe):
            pe.wait_ge(ident_ready, 9)
            pe.wait_ge(weight_loaded, 16 * 8)
            for w in range(4):
                last = nc.tensor.transpose(pa[:, w * P:(w + 1) * P], weight_in[:, w, :], ident[:])
            last.then_inc(weight_turned, 1)
            pe.wait_ge(plan_cols, 1)
            nc.tensor.transpose(pb[:, 0:COARSE], dcol[:COARSE, :], ident[:COARSE, :COARSE]).then_inc(plan_turned, 1)
            pe.wait_ge(weight_ready, 1)
            pe.wait_ge(coarse_ready, 1)

            def edge_turn_features(b, k, t):
                pe.wait_ge(ea_loaded[k], 16 * (t + 1))
                pe.wait_ge(msgT_ready, over(msgT_ready, b))
                for q in range(J // 2):
                    done = nc.tensor.transpose(pa[:, q * P:(q + 1) * P], pair_of(ea[k], q), ident[:])
                done.then_inc(e_turned, 1)

            def edge_turn_rows(b, k, t):
                pe.wait_ge(g_h, b + 1)
                pe.wait_ge(eaT_ready, b + 1)
                for q in range(J // 2):
                    done = nc.tensor.transpose(pa[:, q * P:(q + 1) * P], pair_of(hg, q), ident[:])
                done.then_inc(h_turned, 1)

            def edge_message(b, k, t):
                pe.wait_ge(hgT_ready, b + 1)
                nc.tensor.matmul(pa[:, :], weight[:, MH, :], hgT[:], start=True, stop=False)
                nc.tensor.matmul(pa[:, :], weight[:, ME, :], eaT[:], start=False, stop=True).then_inc(g_msg, 1)

            def edge_update(b, k, t):
                pe.wait_ge(msgT_ready, over(msgT_ready, b + 1))
                pe.wait_ge(ys_ready, over(ys_ready, 2 * b))
                for q in range(J // 2):
                    done = nc.tensor.matmul(pb[:, q * P:(q + 1) * P], msgT[:, q * P:(q + 1) * P], weight[:, UZ, :], start=True, stop=True)
                done.then_inc(g_update, 1)

            def edge_products(b, k, t):
                for part in (edge_turn_features, edge_turn_rows, edge_message, edge_update):
                    part(b, k, t)

            edge_products(*edges(0, 0))
            edge_products(*edges(0, 1))
            pe.wait_ge(unfit_ready, 1)
            pe.wait_ge(ys_ready, over(ys_ready, 2 * 2))
            nc.tensor.matmul(pb[0:1, 0:1], unfit_sum[:], ones[:], start=True, stop=True).then_inc(unfit_counted, 1)
            pe.wait_ge(general_ready, 1)
            edge_products(*edges(0, 2))

            def turn_rows(i, m):
                n, _ = chunk(i, m)
                pe.wait_ge(n_h, over(n_h, n + 1))
                for h in range(2):
                    pe.wait_ge(hT_ready, over(hT_ready, 2 * n - 1 + h))
                    for q in range(G // 2):
                        done = nc.tensor.transpose(turned[h][:, q * P:(q + 1) * P], pair_of(xc[m % 2], h * G // 2 + q), ident[:])
                    done.then_inc(n_turned, 1)

            def products(i, m, windows):
                n, _ = chunk(i, m)
                if windows:
                    pe.wait_ge(hit_ready, n + 1)
                else:
                    pe.wait_ge(win_loaded[m % NX], 16 * (turns(i, m) + 1))
                for h in range(2):
                    pe.wait_ge(hT_ready, over(hT_ready, 2 * n + h + 1))
                    pe.wait_ge(pre_read[m % 2], over(pre_read[m % 2], 2 * before(i, m) - 1 + h))
                    for q in range(G // 2):
                        g = h * G // 2 + q
                        part = pre[m % 2][h][:, q * P:(q + 1) * P]
                        nc.tensor.matmul(part, hT[m % 2][:, h, q * P:(q + 1) * P], weight[:, UH, :], start=True, stop=False)
                        if windows:
                            done = nc.tensor.matmul(part, hit[m % 2][:WINDOW + 1, g, :], win[m % NX][:WINDOW + 1, g, 0:2 * D], start=False, stop=True)
                        else:
                            done = nc.tensor.matmul(part, ident[:], win[m % NX][:, g, 0:2 * D], start=False, stop=True)
                    done.then_inc(pre_ready, 1)

            def pair(i, m, b, prev, windows):
                begins, ends = isinstance(i, int) and m == 0, isinstance(i, int) and m == CHUNKS
                if b:
                    edge_turn_features(*b)
                if not begins:
                    products(i, m - 1, windows)
                if b:
                    edge_turn_rows(*b)
                turn_rows(i, m)
                if b:
                    edge_message(*b)
                    edge_update(*b)
                products(i, m, windows)
                if not ends:
                    turn_rows(i, m + 1)

            def slow():
                blocks_alone(pe, edge_products)
                with pe.Fori(0, TILES) as t:
                    pe.wait_ge(y_cols, t + 1)
                    nc.tensor.transpose(pa[:, 0:P], dcol[:], ident[:]).then_inc(y_rows, 1)
                    pe.wait_ge(y_same, t + 1)
                    nc.tensor.matmul(pb[:, 0:2 * D], same[:], yt[:, 0:2 * D], start=True, stop=True).then_inc(y_sum, 1)
                pairs(pe, pair, False)

            both_ways(pe, lambda: pairs(pe, pair, True), slow)


_INS = ["x", "src", "dst", "edge_attr_64", "L0_gnn_M_W", "L0_gnn_M_b", "L0_gnn_U_W", "L0_gnn_U_b"]


def kernel(**inputs):
    import numpy as _np
    import concourse.bacc as _bacc
    from concourse.bass_utils import run_bass_kernel_spmd as _run

    nc = _bacc.Bacc("TRN2", target_bir_lowering=False, num_devices=1)
    arrays, args = {}, []
    for name in _INS:
        a = _np.ascontiguousarray(inputs[name])
        arrays[f"in_{name}"] = a
        args.append(nc.dram_tensor(f"in_{name}", a.shape, mybir.dt.from_np(a.dtype), kind="ExternalInput").ap())
    out = nc.dram_tensor("out_dram", inputs["x"].shape, F32, kind="ExternalOutput").ap()
    gnn_kernel(nc, *args, out)
    r = _run(nc, [arrays], core_ids=[0])
    return r.results[0]["out_dram"]
```

```python
import concourse.bass as bass
from concourse import mybir
from concourse.alu_op_type import AluOpType as ALU
from contextlib import ExitStack

F32 = mybir.dt.float32
I32 = mybir.dt.int32
ACT = mybir.ActivationFunctionType
AX = mybir.AxisListType

P = 128
D = 64
EPS = 1e-5


def gnn_kernel(nc, x, src, dst, edge_attr, M_W, M_b, U_W, U_b, out):
    N = x.shape[0]
    E = src.shape[0]

    G = 8
    GROUP = 2 * P
    CHUNK = G * GROUP
    CHUNKS = N // CHUNK
    HEAD = N - CHUNKS * CHUNK
    HEAD_G = HEAD // GROUP
    HEAD_P = (HEAD - HEAD_G * GROUP) // 2
    R = 2 * G
    HALF = R // 2 * D
    NX = 4
    PAIRS = CHUNKS // 2
    assert CHUNKS % NX == 0 and HEAD % 2 == 0

    J = 8
    BLOCK = P * J
    BLOCKS = -(-E // BLOCK)
    REST_P = (E - (BLOCKS - 1) * BLOCK) // J
    LAG = 3
    assert HEAD_G >= G // 2 and HEAD_G < G
    assert REST_P * J == E - (BLOCKS - 1) * BLOCK and BLOCKS % 2 == 1 and LAG % 2 == 1
    assert PAIRS - 1 + 2 == BLOCKS and (BLOCKS - LAG - 2) % 2 == 0

    HALF_AT, NODE_AT, YW = 2 * D, 2 * D + 1, 2 * D + 4
    WINDOW = 112
    TILES = -(-E // P)
    FAR = 1 << 20

    FINE = 200
    COARSE = E // FINE
    Q = (CHUNKS + 1) * G // 4
    assert COARSE * FINE == E and COARSE <= P and Q <= P
    assert E + WINDOW <= BLOCKS * BLOCK

    ctx = ExitStack()
    with ctx:
        def sb(name, shape, dt=F32):
            return ctx.enter_context(nc.sbuf_tensor(name, shape, dt))

        given = []

        def sem(name, n=0):
            s = ctx.enter_context(nc.semaphore(name))
            if n:
                given.append((s, n))
            return s

        def over(s, n):
            return n + sum(g for t, g in given if t is s)

        messages = nc.dram_tensor("messages", [BLOCKS * BLOCK, YW], F32, kind="Internal").ap()
        table = nc.dram_tensor("table", [(CHUNKS + 1) * CHUNK, D], F32, kind="Internal").ap()
        first_dram = nc.dram_tensor("first_dram", [4 * Q], I32, kind="Internal").ap()

        column = sb("column", [P, P])
        row = sb("row", [P, 1])
        slot = sb("slot", [P, G, P])
        ident = sb("ident", [P, P])
        below = sb("below", [P, P])
        ones = sb("ones", [P, 1])
        eps_t = sb("eps_t", [P, 1])
        weight_in = sb("weight_in", [P, 4, P])
        weight = sb("weight", [P, 4, P])
        MH, ME, UH, UZ = range(4)
        msg_bias = sb("msg_bias", [P, 1])
        node_bias = sb("node_bias", [P, R * D])
        node_bias_row = sb("node_bias_row", [P, D])

        dst_rows = sb("dst_rows", [P, FINE], I32)
        dst_next = sb("dst_next", [P, FINE], I32)
        falls = sb("falls", [P, FINE])
        begin_i = sb("begin_i", [P, 5], I32)
        begin = sb("begin", [P, 5])
        allowed_i = sb("allowed_i", [P, 2], I32)
        allowed = sb("allowed", [P, 1])
        row_starts = sb("row_starts", [P, P])
        coarse_less = sb("coarse_less", [P, 5, COARSE])
        coarse = sb("coarse", [P, 5])
        coarse_i = sb("coarse_i", [P, 5], I32)
        fine = sb("fine", [P, 5, FINE], I32)
        fine_less = sb("fine_less", [P, 5, FINE])
        within = sb("within", [P, 5])
        first = sb("first", [P, 5])
        first_i = sb("first_i", [P, 4], I32)
        first_row = sb("first_row", [1, 4 * Q], I32)
        wide = sb("wide", [P, 4])
        unfit = sb("unfit", [P, 7])
        unfit_sum = sb("unfit_sum", [P, 1])
        general = sb("general", [1, 1], I32)

        xs = [sb(f"xs{k}", [P, R, D]) for k in range(NX)]
        win = [sb(f"win{k}", [P, G, YW]) for k in range(NX)]
        xc = [sb(f"xc{k}", [P, R, D]) for k in range(2)]
        sq = sb("sq", [P, R, D])
        total = sb("total", [P, R])
        var = sb("var", [P, R])
        dev = sb("dev", [P, R])
        rdev = [sb(f"rdev{k}", [P, R]) for k in range(2)]
        base = sb("base", [P, 1])
        hit = [sb(f"hit{k}", [P, G, P]) for k in range(2)]
        hT = [sb(f"hT{k}", [P, 2, HALF]) for k in range(2)]
        res = [sb(f"res{k}", [P, R, D]) for k in range(2)]

        src_all = sb("src_all", [P, BLOCKS, J], I32)
        dst_all = sb("dst_all", [P, BLOCKS, J], I32)
        half_i = sb("half_i", [P, BLOCKS, J], I32)
        odd_i = sb("odd_i", [P, BLOCKS, J], I32)
        number_all = sb("number_all", [P, BLOCKS, J, 2])
        side_all = sb("side_all", [P, BLOCKS, J, 2])
        src_i = [sb(f"src_i{k}", [P, J], I32) for k in range(2)]
        side = [sb(f"side{k}", [P, J, 2]) for k in range(2)]
        xg = [sb(f"xg{k}", [P, J, D]) for k in range(2)]
        ea = [sb(f"ea{k}", [P, J, D]) for k in range(2)]
        hg = sb("hg", [P, J, D])
        sqg = sb("sqg", [P, J, D])
        total_g = sb("total_g", [P, J])
        var_g = sb("var_g", [P, J])
        dev_g = sb("dev_g", [P, J])
        rdev_g = sb("rdev_g", [P, J])
        hgT = sb("hgT", [P, J * D])
        eaT = sb("eaT", [P, J * D])
        msgT = sb("msgT", [P, J * D])
        ys = [sb(f"ys{k}", [P, J, YW]) for k in range(2)]

        yt = sb("yt", [P, YW])
        dcol = sb("dcol", [P, P])
        same = sb("same", [P, P])
        earlier = sb("earlier", [P, P])
        n_before = sb("n_before", [P, 1])
        at_f = sb("at_f", [P, 1])
        read_i = sb("read_i", [P, 1], I32)
        write_i = sb("write_i", [P, 1], I32)
        t_old = sb("t_old", [P, D])
        t_half = sb("t_half", [P, D])
        t_new = sb("t_new", [P, D])

        bank = [ctx.enter_context(nc.psum_tensor(f"bank{k}", [P, 512], F32)) for k in range(8)]
        turned = bank[0:2]
        pre = [bank[2:4], bank[4:6]]
        pa, pb = bank[6], bank[7]

        went = sem("went")

        const_ready = sem("const_ready")
        ident_ready = sem("ident_ready")
        weight_cleared = sem("weight_cleared")
        weight_loaded = sem("weight_loaded")
        weight_turned = sem("weight_turned")
        weight_ready = sem("weight_ready")
        bias_loaded = sem("bias_loaded")
        node_bias_loaded = sem("node_bias_loaded")
        bias_rows = sem("bias_rows")
        bias_ready = sem("bias_ready")
        table_filled = sem("table_filled")

        rows_loaded = sem("rows_loaded")
        next_loaded = sem("next_loaded")
        plan_const = sem("plan_const")
        plan_step = sem("plan_step")
        plan_cols = sem("plan_cols")
        plan_turned = sem("plan_turned")
        coarse_ready = sem("coarse_ready")
        fine_loaded = sem("fine_loaded")
        first_ready = sem("first_ready")
        first_stored = sem("first_stored")
        first_loaded = sem("first_loaded")
        unfit_ready = sem("unfit_ready")
        unfit_counted = sem("unfit_counted")
        general_ready = sem("general_ready")

        index_cleared = sem("index_cleared")
        index_loaded = [sem(f"index_loaded{k}") for k in range(2)]
        numbers_ready = sem("numbers_ready")
        src_ready = sem("src_ready")
        ea_loaded = [sem(f"ea_loaded{k}") for k in range(2)]
        gathered = [sem(f"gathered{k}") for k in range(2)]
        g_total = sem("g_total")
        g_centred = sem("g_centred")
        g_squared = sem("g_squared")
        g_side = sem("g_side")
        g_number = sem("g_number")
        g_var = sem("g_var")
        g_dev = sem("g_dev")
        g_rdev = sem("g_rdev")
        g_h = sem("g_h")
        e_turned = sem("e_turned")
        h_turned = sem("h_turned", 1)
        eaT_ready = sem("eaT_ready")
        hgT_ready = sem("hgT_ready")
        g_msg = sem("g_msg")
        msgT_ready = sem("msgT_ready", 1)
        g_update = sem("g_update")
        ys_ready = sem("ys_ready", 2)
        ys_stored = [sem(f"ys_stored{k}", 16) for k in range(2)]

        y_loaded = sem("y_loaded")
        y_cols = sem("y_cols")
        y_rows = sem("y_rows")
        y_same = sem("y_same")
        y_earlier = sem("y_earlier")
        y_before = sem("y_before")
        y_at = sem("y_at")
        y_read = sem("y_read")
        y_write = sem("y_write")
        y_sum = sem("y_sum")
        t_cleared = sem("t_cleared")
        t_read = sem("t_read")
        t_halfway = sem("t_halfway")
        t_summed = sem("t_summed")
        t_written = sem("t_written")

        x_loaded = [sem(f"x_loaded{k}") for k in range(NX)]
        win_loaded = [sem(f"win_loaded{k}") for k in range(NX)]
        n_total = sem("n_total")
        n_centred = sem("n_centred")
        n_squared = sem("n_squared")
        n_var = sem("n_var", 1)
        n_dev = sem("n_dev")
        n_rdev = sem("n_rdev")
        n_h = sem("n_h", 2)
        n_base = sem("n_base")
        hit_ready = sem("hit_ready")
        n_turned = sem("n_turned", 4)
        hT_ready = sem("hT_ready", 2)
        pre_ready = sem("pre_ready", 8)
        even_ready = sem("even_ready", 2)
        odd_ready = sem("odd_ready", 1)
        odd_relu = sem("odd_relu", 1)
        odd_added = sem("odd_added")
        stored = [sem(f"stored{k}", 16) for k in range(2)]

        def node_rows(t, begin):
            return t[bass.ds(begin, CHUNK), :].rearrange("(g p i) d -> p g (i d)", g=G, i=2)

        def by_group(tile):
            return tile[:].rearrange("p (g i) d -> p g (i d)", i=2)

        def spread(stat, n):
            return stat[:].unsqueeze(2).to_broadcast([P, n, D])

        def pair_of(tile, q):
            return tile[:, 2 * q:2 * q + 2, :].rearrange("p i d -> p (i d)")

        def edges(i, m):
            return 2 * i + m, m % 2, i + m // 2

        def chunk(i, m):
            return NX * i + m, m

        def turns(i, m):
            return i + m // NX

        def before(i, m):
            return 2 * i + m // 2

        def chunk_begin(i, m):
            return 0 if isinstance(i, int) and NX * i + m == CHUNKS else HEAD + (NX * i + m) * CHUNK

        def wait_alone(engine, s, value):
            engine.wait_ge(s, value)
            engine.sem_inc(went, 1)

        def both_ways(engine, fast, slow):
            engine.wait_ge(general_ready, 1)
            unfits = engine.value_load(general[0:1, 0:1], min_val=0, max_val=1)
            with engine.If(unfits == 0):
                fast()
            with engine.Else():
                slow()

        def blocks_alone(engine, step):
            with engine.Fori(0, (BLOCKS - LAG) // 2) as i:
                for k in range(2):
                    step(*edges(i, LAG + k))

        def pairs(engine, pair, windows):
            def block_of(i, m):
                there = windows and not (isinstance(i, int) and LAG + 2 * i + m // 2 >= BLOCKS)
                return edges(i, LAG + m // 2) if there else None
            pair(0, 0, block_of(0, 0), edges(0, LAG - 1) if windows else None, windows)
            loops = (BLOCKS - LAG - 1) // 2
            with engine.Fori(0, loops) as i:
                for m in (2, 4):
                    pair(i, m, block_of(i, m), block_of(i, m - 2), windows)
            for j in range(2 * loops + 1, PAIRS):
                pair(0, 2 * j, block_of(0, 2 * j), block_of(0, 2 * j - 2), windows)
            pair(0, CHUNKS, None, None, windows)

        block = ctx.enter_context(nc.Block())

        @block.sync
        def _(sp):
            for s, n in given:
                sp.sem_inc(s, n)

            def by_edge(dram, b, n, m=P):
                return dram[b * BLOCK:b * BLOCK + n * m * J].rearrange("(b p j) -> p b j", p=m, j=J)

            def load_edges(b, k, t, n=P):
                if t is not None:
                    wait_alone(sp, e_turned, b - 1)
                sp.dma_start(ea[k][:n, :, :], edge_attr[bass.ds(b * BLOCK, n * J), :].rearrange("(p j) d -> p j d", j=J)).then_inc(ea_loaded[k], 16)

            def load_numbers(dram, tile, k):
                b, n = ((0, LAG), (LAG, BLOCKS - 1 - LAG))[k]
                sp.dma_start(tile[:, b:b + n, :], by_edge(dram, b, n)).then_inc(index_loaded[k], 16)
                if k == 1:
                    sp.dma_start(tile[:REST_P, BLOCKS - 1:BLOCKS, :], by_edge(dram, BLOCKS - 1, 1, REST_P)).then_inc(index_loaded[1], 16)

            def load_x(n):
                sp.dma_start(by_group(xs[n]), node_rows(x, HEAD + n * CHUNK)).then_inc(x_loaded[n], 16)

            sp.wait_ge(index_cleared, 2)
            load_numbers(src, src_all, 0)
            sp.dma_start(dst_rows[:COARSE, :], dst.rearrange("(r c) -> r c", c=FINE)).then_inc(rows_loaded, 16)
            load_numbers(dst, dst_all, 0)
            sp.wait_ge(weight_cleared, 1)
            for w, (m, at) in enumerate([(M_W, 0), (M_W, D), (U_W, 0), (U_W, D)]):
                for h in (0, D):
                    sp.dma_start(weight_in[h:h + D, w, h:h + D], m[:, at:at + D]).then_inc(weight_loaded, 16)
            load_edges(0, 0, None)
            load_x(0)
            for h in (0, D):
                sp.dma_start(msg_bias[h:h + D, :], M_b.rearrange("(p a) -> p a", a=1)).then_inc(bias_loaded, 16)
            load_edges(1, 1, None)
            load_x(1)
            sp.dma_start(dst_next[:COARSE - 1, :], dst[1:1 + (COARSE - 1) * FINE].rearrange("(r c) -> r c", c=FINE)).then_inc(next_loaded, 16)
            sp.dma_start(dst_next[COARSE - 1:COARSE, 0:FINE - 1], dst[1 + (COARSE - 1) * FINE:E].rearrange("(r c) -> r c", r=1)).then_inc(next_loaded, 16)
            load_numbers(src, src_all, 1)
            load_numbers(dst, dst_all, 1)
            load_edges(2, 0, 1)
            load_x(2)
            load_x(3)
            sp.dma_start(node_bias_row[:], U_b.rearrange("(a d) -> a d", a=1).to_broadcast([P, D])).then_inc(node_bias_loaded, 16)
            for k in range(NX):
                for h in (0, D):
                    sp.dma_start(win[k][WINDOW:WINDOW + 1, :, h:h + D],
                                 U_b.rearrange("(a b d) -> a b d", a=1, b=1).to_broadcast([1, G, D])).then_inc(bias_rows, 16)
            load_edges(3, 1, 1)
            sp.wait_ge(first_ready, 1)
            sp.dma_start(first_dram.rearrange("(q s) -> q s", s=4), first_i[:Q, :]).then_inc(first_stored, 16)
            sp.wait_ge(first_stored, 16)
            sp.dma_start(first_row[:], first_dram.rearrange("(a q) -> a q", a=1)).then_inc(first_loaded, 16)
            sp.wait_ge(first_loaded, 16)

            def load_windows(i, m):
                n, _ = chunk(i, m)
                _, starts = nc.values_load_multi_w_load_instructions(
                    first_row[0:1, bass.ds(n * G, G)], engines=[sp.engine], min_val=0, max_val=E,
                    skip_runtime_bounds_check_because="they count edges, so are 0 to E, and messages has a window behind them")
                if isinstance(i, int) and n == CHUNKS:
                    slots = (BLOCKS // 2 + 1, BLOCKS // 2)
                else:
                    slots = i + (m // 2 + 1) // 2 + 1, i + (m // 2 + 2) // 2
                for k in range(2):
                    wait_alone(sp, ys_stored[k], over(ys_stored[k], 16 * slots[k]))
                wait_alone(sp, pre_ready, over(pre_ready, 2 * (n - 3)))
                for g in range(G):
                    sp.dma_start(win[m % NX][:WINDOW, g, :], messages[bass.ds(starts[g], WINDOW), :]).then_inc(win_loaded[m % NX], 16)

            def fast():
                def edges_and_windows(i, m, next_block, last):
                    if next_block:
                        b, k, t = next_block
                        load_edges(b, k, t, REST_P if last else P)
                    load_windows(i, m)
                    load_windows(i, m + 1)
                sp.wait_ge(bias_rows, 16 * 2 * NX)
                loops = (BLOCKS - 1 - LAG - 2) // 2 - 1
                load_windows(0, 0)
                load_edges(*edges(0, LAG + 1))
                load_windows(0, 1)
                with sp.Fori(0, loops) as i:
                    for m in (2, 4):
                        edges_and_windows(i, m, edges(i, LAG + 1 + m // 2), False)
                for j in range(2 * loops + 1, PAIRS):
                    b = LAG + 1 + j
                    edges_and_windows(0, 2 * j, edges(0, b) if b < BLOCKS else None, b == BLOCKS - 1)
                load_windows(0, CHUNKS)

            def slow():
                load_edges(*edges(0, LAG + 1))
                with sp.Fori(0, (BLOCKS - LAG - 3) // 2) as i:
                    for k in range(2):
                        load_edges(*edges(i, LAG + 2 + k))
                for b in range(LAG + 2 + 2 * ((BLOCKS - LAG - 3) // 2), BLOCKS):
                    load_edges(*edges(0, b), REST_P if b == BLOCKS - 1 else P)
                sp.wait_ge(bias_ready, 1)
                for c in range(CHUNKS + 1):
                    sp.dma_start(table[c * CHUNK:(c + 1) * CHUNK, :].rearrange("(p r) d -> p (r d)", p=P), node_bias[:]).then_inc(table_filled, 16)
                sp.wait_ge(ys_stored[0], over(ys_stored[0], 16 * (BLOCKS // 2 + 1)))
                sp.wait_ge(ys_stored[1], over(ys_stored[1], 16 * (BLOCKS // 2)))
                sp.wait_ge(table_filled, 16 * (CHUNKS + 1))
                sp.dma_start(yt[:], messages[0:P, :]).then_inc(y_loaded, 16)
                with sp.Fori(1, TILES) as t:
                    wait_alone(sp, t_written, 16 * t)
                    sp.dma_start(yt[:], messages[bass.ds(t * P, P), :]).then_inc(y_loaded, 16)
                sp.wait_ge(t_written, 16 * TILES)
                sp.wait_ge(bias_rows, 16 * 2 * NX)

                def load_table(i, m):
                    n, _ = chunk(i, m)
                    wait_alone(sp, pre_ready, over(pre_ready, 2 * (n - 3)))
                    sp.dma_start(win[m % NX][:, :, 0:2 * D], node_rows(table, chunk_begin(i, m))).then_inc(win_loaded[m % NX], 16)

                with sp.Fori(0, CHUNKS // NX) as i:
                    for m in range(NX):
                        load_table(i, m)
                load_table(0, CHUNKS)

            both_ways(sp, fast, slow)

        @block.gpsimd
        def _(pool):
            nc.gpsimd.memset(src_all[:], 0).then_inc(index_cleared, 1)
            nc.gpsimd.memset(dst_all[:], FAR).then_inc(index_cleared, 1)
            nc.gpsimd.memset(weight_in[:], 0.0).then_inc(weight_cleared, 1)
            nc.gpsimd.iota(column[:], pattern=[[1, P]], base=0, channel_multiplier=0, allow_small_or_imprecise_dtypes=True).then_inc(const_ready, 1)
            nc.gpsimd.iota(row[:], pattern=[[0, 1]], base=0, channel_multiplier=1, allow_small_or_imprecise_dtypes=True).then_inc(const_ready, 1)
            nc.gpsimd.iota(begin_i[:], pattern=[[GROUP, 5]], base=HEAD, channel_multiplier=4 * GROUP).then_inc(plan_const, 1)
            nc.gpsimd.iota(allowed_i[:], pattern=[[0, 2]], base=0, channel_multiplier=1).then_inc(plan_const, 1)

            def gather(b, k, t, used=True):
                if used:
                    wait_alone(pool, gathered[k], 16 * J * t)
                nc.gpsimd.tensor_copy(src_i[k][:], src_all[:, b, :] if isinstance(b, int) else src_all[:, bass.ds(b, 1), :].rearrange("p b j -> p (b j)")).then_inc(src_ready, 1)
                if used:
                    wait_alone(pool, g_centred, b - 1)
                wait_alone(pool, src_ready, b + 1)
                for j in range(J):
                    pool.indirect_dma_start(out=xg[k][:, j, :], out_offset=None, in_=x[:, :],
                                            in_offset=bass.IndirectOffsetOnAxis(ap=src_i[k][:, j:j + 1], axis=0)).then_inc(gathered[k], 16)

            pool.wait_ge(index_loaded[0], 32)
            gather(*edges(0, 0), False)
            nc.gpsimd.iota(slot[:], pattern=[[P, G], [1, P]], base=0, channel_multiplier=0, allow_small_or_imprecise_dtypes=True).then_inc(const_ready, 1)
            gather(*edges(0, 1), False)
            pool.wait_ge(coarse_ready, 1)
            for s in range(5):
                pool.indirect_dma_start(out=fine[:Q, s, :], out_offset=None, in_=dst.rearrange("(r c) -> r c", c=FINE),
                                        in_offset=bass.IndirectOffsetOnAxis(ap=coarse_i[:Q, s:s + 1], axis=0)).then_inc(fine_loaded, 16)
            gather(*edges(0, 2))
            pool.wait_ge(index_loaded[1], 64)
            gather(*edges(0, LAG))

            def scale(i, m):
                n, _ = chunk(i, m)
                pool.wait_ge(n_rdev, n + 1)
                nc.gpsimd.tensor_tensor(xc[m % 2][:], xc[m % 2][:], spread(rdev[m % 2], R), ALU.mult).then_inc(n_h, 1)

            def add_rows(i, m):
                pool.wait_ge(odd_relu, over(odd_relu, before(i, m) + 1))
                nc.gpsimd.tensor_tensor(res[1][:, G:R, :], res[1][:, G:R, :], xs[m % NX][:, G:R, :], ALU.add).then_inc(odd_added, 1)

            def pair(i, m, b, prev, windows):
                begins, ends = isinstance(i, int) and m == 0, isinstance(i, int) and m == CHUNKS
                if b and not (isinstance(i, int) and b[0] == BLOCKS - 1):
                    gather(*edges(i, LAG + 1 + m // 2))
                if begins:
                    return
                scale(i, m)
                add_rows(i, m - 1)
                if not ends:
                    scale(i, m + 1)

            def slow():
                alone = BLOCKS - LAG - 1
                with pool.Fori(0, alone // 2) as i:
                    for k in range(2):
                        gather(*edges(i, LAG + 1 + k))
                gather(*edges(0, BLOCKS - 1))
                nc.gpsimd.memset(t_old[:], 0.0).then_inc(t_cleared, 1)
                pool.wait_ge(t_cleared, 1)
                with pool.Fori(0, TILES) as t:
                    wait_alone(pool, y_read, t + 1)
                    pool.indirect_dma_start(out=t_old[:], out_offset=None, in_=table[:, :],
                                            in_offset=bass.IndirectOffsetOnAxis(ap=read_i[:], axis=0),
                                            bounds_check=N - 1, oob_is_err=False).then_inc(t_read, 16)
                    wait_alone(pool, t_summed, t + 1)
                    wait_alone(pool, y_write, t + 1)
                    pool.indirect_dma_start(out=table[:, :], out_offset=bass.IndirectOffsetOnAxis(ap=write_i[:], axis=0),
                                            in_=t_new[:], in_offset=None,
                                            bounds_check=N - 1, oob_is_err=False).then_inc(t_written, 16)
                pairs(pool, pair, False)

            both_ways(pool, lambda: pairs(pool, pair, True), slow)

        @block.vector
        def _(dve):
            dve.wait_ge(const_ready, 2)
            nc.vector.tensor_scalar(ident[:], column[:], row[:], None, ALU.is_equal).then_inc(ident_ready, 1)
            nc.vector.memset(eps_t[:], EPS).then_inc(ident_ready, 1)
            nc.vector.memset(ones[:], 1.0).then_inc(ident_ready, 1)
            nc.vector.tensor_scalar(below[:], column[:], row[:], None, ALU.is_lt).then_inc(ident_ready, 1)
            for k in range(2):
                nc.vector.memset(hit[k][:], 1.0).then_inc(ident_ready, 1)
                nc.vector.memset(ys[k][:], 0.0).then_inc(ident_ready, 1)
            nc.vector.memset(base[:], float(HEAD // 2)).then_inc(n_base, 1)
            nc.vector.memset(unfit[:], 0.0).then_inc(ident_ready, 1)
            dve.wait_ge(ident_ready, 9)

            steps = []

            def step(instruction):
                steps.append(instruction.then_inc(plan_step, 1))
                dve.wait_ge(plan_step, len(steps))

            def number_blocks(b, n):
                part = slice(b, b + n)
                step(nc.vector.tensor_single_scalar(half_i[:, part, :], dst_all[:, part, :], 1, ALU.logical_shift_right))
                step(nc.vector.tensor_single_scalar(odd_i[:, part, :], dst_all[:, part, :], 1, ALU.bitwise_and))
                step(nc.vector.tensor_copy(number_all[:, part, :, 0:1], half_i[:, part, :].unsqueeze(3)))
                step(nc.vector.tensor_copy(number_all[:, part, :, 1:2], dst_all[:, part, :].unsqueeze(3)))
                step(nc.vector.tensor_scalar(side_all[:, part, :, 0:1], odd_i[:, part, :].unsqueeze(3), -1.0, 1.0, ALU.mult, ALU.add))
                nc.vector.tensor_copy(side_all[:, part, :, 1:2], odd_i[:, part, :].unsqueeze(3)).then_inc(numbers_ready, 1)

            def edge_sum(b, k, t):
                dve.wait_ge(gathered[k], 16 * J * (t + 1))
                nc.vector.tensor_reduce(total_g[:], xg[k][:], AX.X, ALU.add).then_inc(g_total, 1)

            def edge_centre(b, k, t):
                dve.wait_ge(g_total, b + 1)
                dve.wait_ge(h_turned, over(h_turned, b))
                nc.vector.scalar_tensor_tensor(out=hg[:], in0=spread(total_g, J), scalar=-1.0 / D, in1=xg[k][:],
                                               op0=ALU.mult, op1=ALU.add).then_inc(g_centred, 1)

            def edge_variance(b, k, t):
                dve.wait_ge(g_squared, b + 1)
                nc.vector.tensor_reduce(var_g[:], sqg[:], AX.X, ALU.add).then_inc(g_var, 1)

            def edge_inverse(b, k, t):
                dve.wait_ge(g_dev, b + 1)
                nc.vector.reciprocal(rdev_g[:], dev_g[:]).then_inc(g_rdev, 1)

            def edge_scale(b, k, t):
                dve.wait_ge(g_rdev, b + 1)
                nc.vector.tensor_tensor(hg[:], hg[:], spread(rdev_g, J), ALU.mult).then_inc(g_h, 1)

            def edge_norm(b, k, t):
                for part in (edge_sum, edge_centre, edge_variance, edge_inverse, edge_scale):
                    part(b, k, t)

            def plan():
                dve.wait_ge(rows_loaded, 16)
                dve.wait_ge(plan_const, 2)
                nc.vector.tensor_copy(dcol[:COARSE, :], dst_rows[:COARSE, 0:1].to_broadcast([COARSE, P])).then_inc(plan_cols, 1)
                step(nc.vector.tensor_copy(begin[:], begin_i[:]))
                odd_q = Q - G // 4
                step(nc.vector.tensor_scalar(allowed[:], row[:], float(odd_q), -float(N), ALU.is_ge, ALU.mult))
                step(nc.vector.tensor_scalar(begin[:], begin[:], allowed[:], None, ALU.add))
                step(nc.vector.tensor_single_scalar(allowed_i[:], allowed_i[:], 2, ALU.logical_shift_right))
                step(nc.vector.tensor_copy(allowed[:], allowed_i[:, 0:1]))
                step(nc.vector.tensor_scalar(allowed[:], allowed[:], float(BLOCK), float(2 * BLOCK - WINDOW), ALU.mult, ALU.add))
                dve.wait_ge(plan_turned, 1)
                step(nc.vector.tensor_copy(row_starts[:, 0:COARSE], pb[:, 0:COARSE]))
                step(nc.vector.tensor_tensor(coarse_less[:], row_starts[:, 0:COARSE].unsqueeze(1).to_broadcast([P, 5, COARSE]),
                                             begin[:].unsqueeze(2).to_broadcast([P, 5, COARSE]), ALU.is_lt))
                step(nc.vector.tensor_reduce(coarse[:], coarse_less[:], AX.X, ALU.add))
                step(nc.vector.tensor_scalar(coarse[:], coarse[:], -1.0, 0.0, ALU.add, ALU.max))
                nc.vector.tensor_copy(coarse_i[:], coarse[:]).then_inc(coarse_ready, 1)

            def plan_end():
                dve.wait_ge(next_loaded, 32)
                step(nc.vector.tensor_tensor(falls[:COARSE, 0:FINE - 1], dst_rows[:COARSE, 0:FINE - 1], dst_next[:COARSE, 0:FINE - 1], ALU.is_gt))
                step(nc.vector.tensor_reduce(unfit[:COARSE, 0:1], falls[:COARSE, 0:FINE - 1], AX.X, ALU.max))
                step(nc.vector.tensor_tensor(falls[:COARSE - 1, FINE - 1:FINE], dst_rows[:COARSE - 1, FINE - 1:FINE], dst_next[:COARSE - 1, FINE - 1:FINE], ALU.is_gt))
                step(nc.vector.tensor_tensor(unfit[:COARSE - 1, 0:1], unfit[:COARSE - 1, 0:1], falls[:COARSE - 1, FINE - 1:FINE], ALU.max))
                dve.wait_ge(fine_loaded, 16 * 5)
                step(nc.vector.tensor_tensor(fine_less[:Q], fine[:Q], begin[:Q].unsqueeze(2).to_broadcast([Q, 5, FINE]), ALU.is_lt))
                step(nc.vector.tensor_reduce(within[:Q], fine_less[:Q], AX.X, ALU.add))
                step(nc.vector.scalar_tensor_tensor(out=first[:Q], in0=coarse[:Q], scalar=float(FINE), in1=within[:Q], op0=ALU.mult, op1=ALU.add))
                nc.vector.tensor_copy(first_i[:Q], first[:Q, 0:4]).then_inc(first_ready, 1)
                step(nc.vector.tensor_scalar(unfit[:Q, 1:2], first[:Q, 3:4], allowed[:Q], None, ALU.is_gt))
                step(nc.vector.tensor_tensor(wide[:Q], first[:Q, 1:5], first[:Q, 0:4], ALU.subtract))
                step(nc.vector.tensor_scalar(unfit[:Q, 2:6], wide[:Q], float(WINDOW), None, ALU.is_gt))
                nc.vector.tensor_reduce(unfit_sum[:], unfit[:, 0:6], AX.X, ALU.max).then_inc(unfit_ready, 1)

            def sum_rows(i, m):
                n, _ = chunk(i, m)
                dve.wait_ge(x_loaded[m % NX], 16 * (turns(i, m) + 1))
                nc.vector.tensor_reduce(total[:], xs[m % NX][:], AX.X, ALU.add).then_inc(n_total, 1)

            def centre(i, m):
                n, _ = chunk(i, m)
                dve.wait_ge(n_total, n + 1)
                dve.wait_ge(n_turned, over(n_turned, 2 * n - 2))
                nc.vector.scalar_tensor_tensor(out=xc[m % 2][:], in0=spread(total, R), scalar=-1.0 / D, in1=xs[m % NX][:],
                                               op0=ALU.mult, op1=ALU.add).then_inc(n_centred, 1)

            def find_hits(i, m):
                n, _ = chunk(i, m)
                odd = isinstance(i, int) and n == CHUNKS
                dve.wait_ge(win_loaded[m % NX], 16 * G * (turns(i, m) + 1))
                dve.wait_ge(pre_ready, over(pre_ready, 2 * n - 2))
                dve.wait_ge(n_base, n + 1)
                nc.vector.scalar_tensor_tensor(out=hit[m % 2][:WINDOW], in0=slot[:WINDOW], scalar=0.0 if odd else base[:WINDOW, 0:1],
                                               in1=win[m % NX][:WINDOW, :, HALF_AT:HALF_AT + 1].to_broadcast([WINDOW, G, P]),
                                               op0=ALU.add, op1=ALU.is_equal).then_inc(hit_ready, 1)

            def move_base(i, m):
                n, _ = chunk(i, m)
                dve.wait_ge(hit_ready, n + 1)
                nc.vector.tensor_scalar(base[:], base[:], float(CHUNK // 2), None, ALU.add).then_inc(n_base, 1)

            def variance(i, m):
                n, _ = chunk(i, m)
                dve.wait_ge(n_squared, n + 1)
                nc.vector.tensor_reduce(var[:], sq[:], AX.X, ALU.add).then_inc(n_var, 1)

            def inverse(i, m):
                n, _ = chunk(i, m)
                dve.wait_ge(n_dev, n + 1)
                dve.wait_ge(n_h, over(n_h, n - 1))
                nc.vector.reciprocal(rdev[m % 2][:], dev[:]).then_inc(n_rdev, 1)

            def finish(i, m):
                n, k = chunk(i, m)[0], m % 2
                dve.wait_ge(stored[k], over(stored[k], 16 * before(i, m)))
                for h in range(2 - k):
                    dve.wait_ge(pre_ready, over(pre_ready, 2 * n + h + 1))
                    half = slice(h * G, (h + 1) * G)
                    nc.vector.scalar_tensor_tensor(out=res[k][:, half, :], in0=pre[k][h][:].rearrange("p (r d) -> p r d", d=D),
                                                   scalar=0.0, in1=xs[m % NX][:, half, :], op0=ALU.max, op1=ALU.add).then_inc(odd_ready if k else even_ready, 1)

            def invert_scale(n):
                inverse(0, n)
                dve.wait_ge(n_rdev, n + 1)
                nc.vector.tensor_tensor(xc[n][:], xc[n][:], spread(rdev[n], R), ALU.mult).then_inc(n_h, 1)

            plan()
            dve.wait_ge(index_loaded[0], 32)
            number_blocks(0, LAG)
            dve.wait_ge(weight_turned, 1)
            nc.vector.tensor_copy(weight[:].rearrange("p w c -> p (w c)"), pa[:, :]).then_inc(weight_ready, 1)
            edge_norm(*edges(0, 0))
            sum_rows(0, 0)
            centre(0, 0)
            variance(0, 0)
            invert_scale(0)
            edge_norm(*edges(0, 1))
            plan_end()
            sum_rows(0, 1)
            centre(0, 1)
            dve.wait_ge(unfit_counted, 1)
            nc.vector.tensor_scalar(general[:], pre[1][1][0:1, 0:1], 1.0, None, ALU.min).then_inc(general_ready, 1)
            edge_sum(*edges(0, 2))
            edge_centre(*edges(0, 2))
            variance(0, 1)
            edge_variance(*edges(0, 2))
            dve.wait_ge(index_loaded[1], 64)
            number_blocks(LAG, BLOCKS - LAG)
            edge_inverse(*edges(0, 2))
            edge_scale(*edges(0, 2))
            invert_scale(1)
            dve.wait_ge(const_ready, 3)

            def pair(i, m, b, prev, windows):
                begins, ends = isinstance(i, int) and m == 0, isinstance(i, int) and m == CHUNKS
                if not begins:
                    sum_rows(i, m)
                if b:
                    edge_sum(*b)
                if not begins:
                    centre(i, m)
                if b:
                    edge_centre(*b)
                if windows and not begins:
                    find_hits(i, m - 1)
                if not begins:
                    variance(i, m)
                if b:
                    edge_variance(*b)
                if windows and not begins:
                    move_base(i, m - 1)
                if not begins:
                    finish(i, m - 2)
                    inverse(i, m)
                if not begins and not ends:
                    sum_rows(i, m + 1)
                if b:
                    edge_inverse(*b)
                if not begins and not ends:
                    centre(i, m + 1)
                if b:
                    edge_scale(*b)
                if not begins:
                    finish(i, m - 1)
                if not begins and not ends:
                    variance(i, m + 1)
                if windows:
                    find_hits(i, m)
                if not begins and not ends:
                    inverse(i, m + 1)
                if windows and not ends:
                    move_base(i, m)
                if ends:
                    finish(i, m)

            def slow():
                dve.wait_ge(node_bias_loaded, 16)
                nc.vector.tensor_copy(node_bias[:].rearrange("p (r d) -> p r d", d=D),
                                      node_bias_row[:].unsqueeze(1).to_broadcast([P, R, D])).then_inc(bias_ready, 1)
                blocks_alone(dve, edge_norm)
                with dve.Fori(0, TILES) as t:
                    dve.wait_ge(y_loaded, 16 * t + 16)
                    nc.vector.tensor_copy(dcol[:], yt[:, NODE_AT:NODE_AT + 1].to_broadcast([P, P])).then_inc(y_cols, 1)
                    nc.vector.tensor_copy(read_i[:], yt[:, NODE_AT:NODE_AT + 1]).then_inc(y_read, 1)
                    dve.wait_ge(y_rows, t + 1)
                    nc.vector.tensor_scalar(same[:], pa[:, 0:P], yt[:, NODE_AT:NODE_AT + 1], None, ALU.is_equal).then_inc(y_same, 1)
                    dve.wait_ge(y_same, t + 1)
                    nc.vector.tensor_tensor(earlier[:], same[:], below[:], ALU.mult).then_inc(y_earlier, 1)
                    dve.wait_ge(y_earlier, t + 1)
                    nc.vector.tensor_reduce(n_before[:], earlier[:], AX.X, ALU.add).then_inc(y_before, 1)
                    dve.wait_ge(y_before, t + 1)
                    nc.vector.tensor_scalar(at_f[:], n_before[:], 0.0, float(FAR), ALU.is_gt, ALU.mult).then_inc(y_at, 1)
                    dve.wait_ge(y_at, t + 1)
                    nc.vector.tensor_tensor(write_i[:], at_f[:], yt[:, NODE_AT:NODE_AT + 1], ALU.add).then_inc(y_write, 1)
                    dve.wait_ge(y_sum, t + 1)
                    dve.wait_ge(t_read, 16 * t + 16)
                    nc.vector.tensor_tensor(t_half[:], pb[:, 0:D], t_old[:], ALU.add).then_inc(t_halfway, 1)
                    dve.wait_ge(t_halfway, t + 1)
                    nc.vector.tensor_tensor(t_new[:], pb[:, D:2 * D], t_half[:], ALU.add).then_inc(t_summed, 1)
                pairs(dve, pair, False)

            both_ways(dve, lambda: pairs(dve, pair, True), slow)

        @block.scalar
        def _(act):
            act.wait_ge(ident_ready, 9)
            act.wait_ge(bias_loaded, 32)

            def edge_square(b, k, t):
                act.wait_ge(g_centred, b + 1)
                nc.scalar.activation(sqg[:], hg[:], ACT.Square, scale=D ** -0.5).then_inc(g_squared, 1)

            def edge_features(b, k, t):
                act.wait_ge(e_turned, b + 1)
                nc.scalar.copy(eaT[:], pa[:, :]).then_inc(eaT_ready, 1)

            def edge_deviation(b, k, t):
                act.wait_ge(g_var, b + 1)
                nc.scalar.activation(dev_g[:], var_g[:], ACT.Sqrt, bias=eps_t[:]).then_inc(g_dev, 1)

            def edge_relu(b, k, t):
                act.wait_ge(h_turned, over(h_turned, b + 1))
                nc.scalar.activation(hgT[:], pa[:, :], ACT.Relu).then_inc(hgT_ready, 1)

            def edge_message(b, k, t):
                act.wait_ge(g_msg, b + 1)
                nc.scalar.activation(msgT[:], pa[:, :], ACT.Relu, bias=msg_bias[:]).then_inc(msgT_ready, 1)

            def edge_numbers(b, k, t):
                act.wait_ge(numbers_ready, 1 if isinstance(b, int) and b < LAG else 2)
                act.wait_ge(ys_stored[k], over(ys_stored[k], 16 * t))
                nc.scalar.copy(ys[k][:, :, HALF_AT:NODE_AT + 1], number_all[:, bass.ds(b, 1), :, :].rearrange("p b j c -> p (b j) c")).then_inc(g_number, 1)
                nc.scalar.copy(side[k][:], side_all[:, bass.ds(b, 1), :, :].rearrange("p b j c -> p (b j) c")).then_inc(g_side, 1)

            def edge_rows(b, k, t, s):
                if s == 0:
                    act.wait_ge(g_update, b + 1)
                    act.wait_ge(g_side, b + 1)
                for j in range(J):
                    done = nc.scalar.activation(ys[k][:, j, s * D:(s + 1) * D], pb[:, j * D:(j + 1) * D], ACT.Identity, scale=side[k][:, j, s:s + 1])
                done.then_inc(ys_ready, 1)

            def edge_store(b, k, t):
                act.wait_ge(ys_ready, over(ys_ready, 2 * b + 2))
                act.wait_ge(g_number, b + 1)
                act.dma_start(messages[bass.ds(b * BLOCK, BLOCK), :].rearrange("(p j) d -> p j d", j=J), ys[k][:]).then_inc(ys_stored[k], 16)

            def edge_copies(b, k, t):
                for part in (edge_features, edge_square, edge_deviation, edge_relu, edge_message):
                    part(b, k, t)
                edge_numbers(b, k, t)
                for s in range(2):
                    edge_rows(b, k, t, s)
                edge_store(b, k, t)

            def square(i, m):
                n, _ = chunk(i, m)
                act.wait_ge(n_centred, n + 1)
                act.wait_ge(n_var, over(n_var, n))
                nc.scalar.activation(sq[:], xc[m % 2][:], ACT.Square, scale=D ** -0.5).then_inc(n_squared, 1)

            def deviation(i, m):
                n, _ = chunk(i, m)
                act.wait_ge(n_var, over(n_var, n + 1))
                nc.scalar.activation(dev[:], var[:], ACT.Sqrt, bias=eps_t[:]).then_inc(n_dev, 1)

            def relu(i, m):
                n, _ = chunk(i, m)
                act.wait_ge(pre_ready, over(pre_ready, 2 * (n - 1)))
                for h in range(2):
                    act.wait_ge(n_turned, over(n_turned, 2 * n + h + 1))
                    nc.scalar.activation(hT[m % 2][:, h, :], turned[h][:], ACT.Relu).then_inc(hT_ready, 1)

            def last_relu(i, m):
                n, _ = chunk(i, m)
                act.wait_ge(stored[1], over(stored[1], 16 * before(i, m)))
                act.wait_ge(pre_ready, over(pre_ready, 2 * n + 2))
                nc.scalar.activation(res[1][:, G:R, :], pre[1][1][:].rearrange("p (r d) -> p r d", d=D), ACT.Relu).then_inc(odd_relu, 1)

            def store(i, m):
                n, _ = chunk(i, m)
                if m % 2:
                    act.wait_ge(odd_ready, over(odd_ready, before(i, m) + 1))
                    act.wait_ge(odd_added, before(i, m) + 1)
                else:
                    act.wait_ge(even_ready, over(even_ready, 2 * before(i, m) + 2))
                act.dma_start(node_rows(out, chunk_begin(i, m)), by_group(res[m % 2])).then_inc(stored[m % 2], 16)
                if not (isinstance(i, int) and n + NX > CHUNKS):
                    act.dma_start(by_group(xs[m % NX]), node_rows(x, chunk_begin(i, m + NX))).then_inc(x_loaded[m % NX], 16)

            b0, b1, b2 = (edges(0, b) for b in range(LAG))
            edge_features(*b0)
            edge_square(*b0)
            edge_deviation(*b0)
            edge_relu(*b0)
            square(0, 0)
            deviation(0, 0)
            edge_message(*b0)
            edge_square(*b1)
            edge_deviation(*b1)
            edge_features(*b1)
            edge_relu(*b1)
            edge_numbers(*b0)
            edge_rows(*b0, 0)
            edge_rows(*b0, 1)
            edge_store(*b0)
            edge_message(*b1)
            edge_numbers(*b1)
            relu(0, 0)
            square(0, 1)
            edge_rows(*b1, 0)
            edge_square(*b2)
            deviation(0, 1)
            edge_rows(*b1, 1)
            edge_deviation(*b2)
            edge_store(*b1)
            edge_features(*b2)
            edge_relu(*b2)

            def pair(i, m, b, prev, windows):
                begins, ends = isinstance(i, int) and m == 0, isinstance(i, int) and m == CHUNKS
                if begins and windows:
                    edge_square(*b)
                    edge_deviation(*b)
                    edge_message(*prev)
                    edge_features(*b)
                    edge_relu(*b)
                    edge_numbers(*prev)
                    edge_rows(*prev, 0)
                    edge_rows(*prev, 1)
                    edge_store(*prev)
                    edge_message(*b)
                    return
                if not begins:
                    square(i, m)
                if prev:
                    edge_numbers(*prev)
                if b:
                    edge_square(*b)
                if prev:
                    edge_rows(*prev, 0)
                if not begins:
                    deviation(i, m)
                if b:
                    edge_deviation(*b)
                if not begins:
                    relu(i, m - 1)
                if prev:
                    edge_rows(*prev, 1)
                if not begins:
                    store(i, m - 2)
                if not begins and not ends:
                    square(i, m + 1)
                if b:
                    edge_features(*b)
                if prev:
                    edge_store(*prev)
                if b:
                    edge_relu(*b)
                if not begins:
                    last_relu(i, m - 1)
                if not begins and not ends:
                    deviation(i, m + 1)
                if not begins:
                    relu(i, m)
                    store(i, m - 1)
                if b:
                    edge_message(*b)

            def store_odd():
                for h, (g0, g1) in enumerate([(0, G // 2), (G // 2, HEAD_G)]):
                    act.wait_ge(even_ready, over(even_ready, 2 * (CHUNKS // 2) + h + 1))
                    act.dma_start(out[g0 * GROUP:g1 * GROUP, :].rearrange("(g p i) d -> p g (i d)", g=g1 - g0, i=2),
                                  by_group(res[0])[:, g0:g1, :]).then_inc(stored[0], 16)
                act.dma_start(out[HEAD_G * GROUP:HEAD, :].rearrange("(p i) d -> p (i d)", i=2),
                              by_group(res[0])[:HEAD_P, HEAD_G, :]).then_inc(stored[0], 16)
                act.wait_ge(stored[0], over(stored[0], 16 * (CHUNKS // 2 + 3)))
                act.wait_ge(stored[1], over(stored[1], 16 * (CHUNKS // 2)))

            def fast():
                pairs(act, pair, True)
                store_odd()

            def slow():
                edge_message(*b2)
                edge_numbers(*b2)
                edge_rows(*b2, 0)
                edge_rows(*b2, 1)
                edge_store(*b2)
                blocks_alone(act, edge_copies)
                pairs(act, pair, False)
                store_odd()

            both_ways(act, fast, slow)

        @block.tensor
        def _(pe):
            pe.wait_ge(ident_ready, 9)
            pe.wait_ge(plan_cols, 1)
            nc.tensor.transpose(pb[:, 0:COARSE], dcol[:COARSE, :], ident[:COARSE, :COARSE]).then_inc(plan_turned, 1)
            pe.wait_ge(weight_loaded, 16 * 8)
            for w in range(4):
                last = nc.tensor.transpose(pa[:, w * P:(w + 1) * P], weight_in[:, w, :], ident[:])
            last.then_inc(weight_turned, 1)
            pe.wait_ge(weight_ready, 1)
            pe.wait_ge(coarse_ready, 1)

            def edge_turn_features(b, k, t):
                pe.wait_ge(ea_loaded[k], 16 * (t + 1))
                pe.wait_ge(msgT_ready, over(msgT_ready, b))
                for q in range(J // 2):
                    done = nc.tensor.transpose(pa[:, q * P:(q + 1) * P], pair_of(ea[k], q), ident[:])
                done.then_inc(e_turned, 1)

            def edge_turn_rows(b, k, t):
                pe.wait_ge(g_h, b + 1)
                pe.wait_ge(eaT_ready, b + 1)
                for q in range(J // 2):
                    done = nc.tensor.transpose(pa[:, q * P:(q + 1) * P], pair_of(hg, q), ident[:])
                done.then_inc(h_turned, 1)

            def edge_message(b, k, t):
                pe.wait_ge(hgT_ready, b + 1)
                nc.tensor.matmul(pa[:, :], weight[:, MH, :], hgT[:], start=True, stop=False)
                nc.tensor.matmul(pa[:, :], weight[:, ME, :], eaT[:], start=False, stop=True).then_inc(g_msg, 1)

            def edge_update(b, k, t):
                pe.wait_ge(msgT_ready, over(msgT_ready, b + 1))
                pe.wait_ge(ys_ready, over(ys_ready, 2 * b))
                for q in range(J // 2):
                    done = nc.tensor.matmul(pb[:, q * P:(q + 1) * P], msgT[:, q * P:(q + 1) * P], weight[:, UZ, :], start=True, stop=True)
                done.then_inc(g_update, 1)

            def edge_products(b, k, t):
                for part in (edge_turn_features, edge_turn_rows, edge_message, edge_update):
                    part(b, k, t)

            def turn_rows(i, m):
                n, _ = chunk(i, m)
                pe.wait_ge(n_h, over(n_h, n + 1))
                for h in range(2):
                    pe.wait_ge(hT_ready, over(hT_ready, 2 * n - 1 + h))
                    for q in range(G // 2):
                        done = nc.tensor.transpose(turned[h][:, q * P:(q + 1) * P], pair_of(xc[m % 2], h * G // 2 + q), ident[:])
                    done.then_inc(n_turned, 1)

            def products(i, m, windows):
                n, _ = chunk(i, m)
                if windows:
                    pe.wait_ge(hit_ready, n + 1)
                else:
                    pe.wait_ge(win_loaded[m % NX], 16 * (turns(i, m) + 1))
                for h in range(2):
                    pe.wait_ge(hT_ready, over(hT_ready, 2 * n + h + 1))
                    if m % 2:
                        read = (odd_ready, odd_relu)[h]
                        pe.wait_ge(read, over(read, before(i, m)))
                    else:
                        pe.wait_ge(even_ready, over(even_ready, 2 * before(i, m) - 1 + h))
                    for q in range(G // 2):
                        g = h * G // 2 + q
                        part = pre[m % 2][h][:, q * P:(q + 1) * P]
                        nc.tensor.matmul(part, hT[m % 2][:, h, q * P:(q + 1) * P], weight[:, UH, :], start=True, stop=False)
                        if windows:
                            done = nc.tensor.matmul(part, hit[m % 2][:WINDOW + 1, g, :], win[m % NX][:WINDOW + 1, g, 0:2 * D], start=False, stop=True)
                        else:
                            done = nc.tensor.matmul(part, ident[:], win[m % NX][:, g, 0:2 * D], start=False, stop=True)
                    done.then_inc(pre_ready, 1)

            edge_products(*edges(0, 0))
            turn_rows(0, 0)
            edge_turn_features(*edges(0, 1))
            edge_turn_rows(*edges(0, 1))
            edge_message(*edges(0, 1))
            pe.wait_ge(unfit_ready, 1)
            nc.tensor.matmul(pre[1][1][0:1, 0:1], unfit_sum[:], ones[:], start=True, stop=True).then_inc(unfit_counted, 1)
            edge_update(*edges(0, 1))
            edge_turn_features(*edges(0, 2))
            edge_turn_rows(*edges(0, 2))
            turn_rows(0, 1)
            edge_message(*edges(0, 2))
            edge_update(*edges(0, 2))

            def pair(i, m, b, prev, windows):
                begins, ends = isinstance(i, int) and m == 0, isinstance(i, int) and m == CHUNKS
                if b:
                    edge_turn_features(*b)
                if not begins:
                    products(i, m - 1, windows)
                if b:
                    edge_turn_rows(*b)
                if not begins:
                    turn_rows(i, m)
                if b:
                    edge_message(*b)
                products(i, m, windows)
                if b:
                    edge_update(*b)
                if not begins and not ends:
                    turn_rows(i, m + 1)

            def slow():
                blocks_alone(pe, edge_products)
                with pe.Fori(0, TILES) as t:
                    pe.wait_ge(y_cols, t + 1)
                    nc.tensor.transpose(pa[:, 0:P], dcol[:], ident[:]).then_inc(y_rows, 1)
                    pe.wait_ge(y_same, t + 1)
                    nc.tensor.matmul(pb[:, 0:2 * D], same[:], yt[:, 0:2 * D], start=True, stop=True).then_inc(y_sum, 1)
                pairs(pe, pair, False)

            both_ways(pe, lambda: pairs(pe, pair, True), slow)


_INS = ["x", "src", "dst", "edge_attr_64", "L0_gnn_M_W", "L0_gnn_M_b", "L0_gnn_U_W", "L0_gnn_U_b"]


def kernel(**inputs):
    import numpy as _np
    import concourse.bacc as _bacc
    from concourse.bass_utils import run_bass_kernel_spmd as _run

    nc = _bacc.Bacc("TRN2", target_bir_lowering=False, num_devices=1)
    arrays, args = {}, []
    for name in _INS:
        a = _np.ascontiguousarray(inputs[name])
        arrays[f"in_{name}"] = a
        args.append(nc.dram_tensor(f"in_{name}", a.shape, mybir.dt.from_np(a.dtype), kind="ExternalInput").ap())
    out = nc.dram_tensor("out_dram", inputs["x"].shape, F32, kind="ExternalOutput").ap()
    gnn_kernel(nc, *args, out)
    r = _run(nc, [arrays], core_ids=[0])
    return r.results[0]["out_dram"]
```
